# Optimizing a Trainium2 kernel written in Bass

```python
import numpy as np
import jax
import jax.numpy as jnp

def _softmax(x, axis=-1):
    return jax.nn.softmax(x, axis=axis)

def _gelu(x):
    return jax.nn.gelu(x, approximate=True)

def _silu(x):
    return jax.nn.silu(x)

def _sigmoid(x):
    return jax.nn.sigmoid(x)

def _layernorm(x, axis=-1, eps=1e-05):
    m = jnp.mean(x, axis=axis, keepdims=True)
    v = jnp.var(x, axis=axis, keepdims=True)
    return (x - m) / jnp.sqrt(v + eps)

def _scatter_add(tgt, idx, src, axis=0):
    return tgt.at[idx].add(src)

def _segment_sum(src, seg, n):
    return jax.ops.segment_sum(src, seg, n)
kernel_name = 'mk_dlrm_tower_d1_rec_r8_53da0d'

def setup_inputs(seed: int=0):
    np.random.seed(seed)
    _w = jnp.asarray

    def _rec_inputs():
        import jax
        import jax.numpy as jnp
        _tk = jax.random.key(seed)
        dense_ctx = jax.random.normal(jax.random.fold_in(_tk, 190), (512, 16), jnp.float32)
        ids = jnp.stack([jax.random.randint(jax.random.fold_in(_tk, 200 + f), (512,), 0, v, jnp.int32) for f, v in enumerate([1250, 1250, 125000, 1250, 12500, 1250, 1000, 12500, 12500, 1250, 1000, 125000, 12500, 1250, 1250, 125000, 125000, 1000, 1250, 1250, 1000, 1000, 1000, 1000, 12500, 1000, 1250, 1000, 1250, 1250, 1250, 1000])], axis=1)
        tbl_0 = 0.05 * jax.random.normal(jax.random.fold_in(_tk, 500 + 0), (1250, 32), jnp.float32)
        tbl_1 = 0.05 * jax.random.normal(jax.random.fold_in(_tk, 500 + 1), (1250, 32), jnp.float32)
        tbl_2 = 0.05 * jax.random.normal(jax.random.fold_in(_tk, 500 + 2), (125000, 32), jnp.float32)
        tbl_3 = 0.05 * jax.random.normal(jax.random.fold_in(_tk, 500 + 3), (1250, 32), jnp.float32)
        tbl_4 = 0.05 * jax.random.normal(jax.random.fold_in(_tk, 500 + 4), (12500, 32), jnp.float32)
        tbl_5 = 0.05 * jax.random.normal(jax.random.fold_in(_tk, 500 + 5), (1250, 32), jnp.float32)
        tbl_6 = 0.05 * jax.random.normal(jax.random.fold_in(_tk, 500 + 6), (1000, 32), jnp.float32)
        tbl_7 = 0.05 * jax.random.normal(jax.random.fold_in(_tk, 500 + 7), (12500, 32), jnp.float32)
        tbl_8 = 0.05 * jax.random.normal(jax.random.fold_in(_tk, 500 + 8), (12500, 32), jnp.float32)
        tbl_9 = 0.05 * jax.random.normal(jax.random.fold_in(_tk, 500 + 9), (1250, 32), jnp.float32)
        tbl_10 = 0.05 * jax.random.normal(jax.random.fold_in(_tk, 500 + 10), (1000, 32), jnp.float32)
        tbl_11 = 0.05 * jax.random.normal(jax.random.fold_in(_tk, 500 + 11), (125000, 32), jnp.float32)
        tbl_12 = 0.05 * jax.random.normal(jax.random.fold_in(_tk, 500 + 12), (12500, 32), jnp.float32)
        tbl_13 = 0.05 * jax.random.normal(jax.random.fold_in(_tk, 500 + 13), (1250, 32), jnp.float32)
        tbl_14 = 0.05 * jax.random.normal(jax.random.fold_in(_tk, 500 + 14), (1250, 32), jnp.float32)
        tbl_15 = 0.05 * jax.random.normal(jax.random.fold_in(_tk, 500 + 15), (125000, 32), jnp.float32)
        tbl_16 = 0.05 * jax.random.normal(jax.random.fold_in(_tk, 500 + 16), (125000, 32), jnp.float32)
        tbl_17 = 0.05 * jax.random.normal(jax.random.fold_in(_tk, 500 + 17), (1000, 32), jnp.float32)
        tbl_18 = 0.05 * jax.random.normal(jax.random.fold_in(_tk, 500 + 18), (1250, 32), jnp.float32)
        tbl_19 = 0.05 * jax.random.normal(jax.random.fold_in(_tk, 500 + 19), (1250, 32), jnp.float32)
        tbl_20 = 0.05 * jax.random.normal(jax.random.fold_in(_tk, 500 + 20), (1000, 32), jnp.float32)
        tbl_21 = 0.05 * jax.random.normal(jax.random.fold_in(_tk, 500 + 21), (1000, 32), jnp.float32)
        tbl_22 = 0.05 * jax.random.normal(jax.random.fold_in(_tk, 500 + 22), (1000, 32), jnp.float32)
        tbl_23 = 0.05 * jax.random.normal(jax.random.fold_in(_tk, 500 + 23), (1000, 32), jnp.float32)
        tbl_24 = 0.05 * jax.random.normal(jax.random.fold_in(_tk, 500 + 24), (12500, 32), jnp.float32)
        tbl_25 = 0.05 * jax.random.normal(jax.random.fold_in(_tk, 500 + 25), (1000, 32), jnp.float32)
        tbl_26 = 0.05 * jax.random.normal(jax.random.fold_in(_tk, 500 + 26), (1250, 32), jnp.float32)
        tbl_27 = 0.05 * jax.random.normal(jax.random.fold_in(_tk, 500 + 27), (1000, 32), jnp.float32)
        tbl_28 = 0.05 * jax.random.normal(jax.random.fold_in(_tk, 500 + 28), (1250, 32), jnp.float32)
        tbl_29 = 0.05 * jax.random.normal(jax.random.fold_in(_tk, 500 + 29), (1250, 32), jnp.float32)
        tbl_30 = 0.05 * jax.random.normal(jax.random.fold_in(_tk, 500 + 30), (1250, 32), jnp.float32)
        tbl_31 = 0.05 * jax.random.normal(jax.random.fold_in(_tk, 500 + 31), (1000, 32), jnp.float32)
        _rk = jax.random.fold_in(_tk, 7)
        W_top1 = 0.0606339 * jax.random.normal(jax.random.fold_in(_tk, 801), (272, 512), jnp.float32)
        W_top2 = 0.0441942 * jax.random.normal(jax.random.fold_in(_tk, 802), (512, 256), jnp.float32)
        W_top3 = 0.0625 * jax.random.normal(jax.random.fold_in(_tk, 803), (256, 1), jnp.float32)
        b_top1 = jnp.zeros((512,), jnp.float32)
        b_top2 = jnp.zeros((256,), jnp.float32)
        return (dense_ctx, ids, tbl_0, tbl_1, tbl_2, tbl_3, tbl_4, tbl_5, tbl_6, tbl_7, tbl_8, tbl_9, tbl_10, tbl_11, tbl_12, tbl_13, tbl_14, tbl_15, tbl_16, tbl_17, tbl_18, tbl_19, tbl_20, tbl_21, tbl_22, tbl_23, tbl_24, tbl_25, tbl_26, tbl_27, tbl_28, tbl_29, tbl_30, tbl_31, W_top1, b_top1, W_top2, b_top2, W_top3)
    dense_ctx, ids, tbl_0, tbl_1, tbl_2, tbl_3, tbl_4, tbl_5, tbl_6, tbl_7, tbl_8, tbl_9, tbl_10, tbl_11, tbl_12, tbl_13, tbl_14, tbl_15, tbl_16, tbl_17, tbl_18, tbl_19, tbl_20, tbl_21, tbl_22, tbl_23, tbl_24, tbl_25, tbl_26, tbl_27, tbl_28, tbl_29, tbl_30, tbl_31, W_top1, b_top1, W_top2, b_top2, W_top3 = _rec_inputs()

    def _L0_rec_setup():
        import jax, jax.numpy as jnp
        import numpy as np
        B, N, K = (256, 32, 32)
        CIN_SIZE = [128, 128]
        key = jax.random.key(seed)
        k1, k2, k3 = jax.random.split(key, 3)
        inputs = jax.random.normal(k1, (B, N, K), dtype=jnp.float32)
        W0 = jax.random.normal(k2, (N * N, CIN_SIZE[0]), dtype=jnp.float32) * 0.04
        W1 = jax.random.normal(k3, (N * CIN_SIZE[0], CIN_SIZE[1]), dtype=jnp.float32) * 0.02
        return {'inputs': inputs, 'W0': W0, 'W1': W1}
    _L0_rec_all = _L0_rec_setup()
    _L0_rec_in = {k: v for k, v in _L0_rec_all.items() if k in ('W0', 'W1')}
    del _L0_rec_all
    return {'dense_ctx': dense_ctx, 'ids': ids, 'tbl_0': tbl_0, 'tbl_1': tbl_1, 'tbl_2': tbl_2, 'tbl_3': tbl_3, 'tbl_4': tbl_4, 'tbl_5': tbl_5, 'tbl_6': tbl_6, 'tbl_7': tbl_7, 'tbl_8': tbl_8, 'tbl_9': tbl_9, 'tbl_10': tbl_10, 'tbl_11': tbl_11, 'tbl_12': tbl_12, 'tbl_13': tbl_13, 'tbl_14': tbl_14, 'tbl_15': tbl_15, 'tbl_16': tbl_16, 'tbl_17': tbl_17, 'tbl_18': tbl_18, 'tbl_19': tbl_19, 'tbl_20': tbl_20, 'tbl_21': tbl_21, 'tbl_22': tbl_22, 'tbl_23': tbl_23, 'tbl_24': tbl_24, 'tbl_25': tbl_25, 'tbl_26': tbl_26, 'tbl_27': tbl_27, 'tbl_28': tbl_28, 'tbl_29': tbl_29, 'tbl_30': tbl_30, 'tbl_31': tbl_31, 'W_top1': W_top1, 'b_top1': b_top1, 'W_top2': W_top2, 'b_top2': b_top2, 'W_top3': W_top3, 'L0_rec_W0': _L0_rec_in['W0'], 'L0_rec_W1': _L0_rec_in['W1']}

def reference(dense_ctx, ids, tbl_0, tbl_1, tbl_2, tbl_3, tbl_4, tbl_5, tbl_6, tbl_7, tbl_8, tbl_9, tbl_10, tbl_11, tbl_12, tbl_13, tbl_14, tbl_15, tbl_16, tbl_17, tbl_18, tbl_19, tbl_20, tbl_21, tbl_22, tbl_23, tbl_24, tbl_25, tbl_26, tbl_27, tbl_28, tbl_29, tbl_30, tbl_31, W_top1, b_top1, W_top2, b_top2, W_top3, L0_rec_W0, L0_rec_W1):
    import jax
    import jax.numpy as jnp

    def _L0_rec_ref(inputs, W0, W1):
        import jax, jax.numpy as jnp
        import numpy as np
        B, N, K = (256, 32, 32)
        CIN_SIZE = [128, 128]
        b, n, k = inputs.shape
        x = inputs
        res = []
        for W in (W0, W1):
            prev = x.shape[1]
            z = jnp.einsum('bhd,bmd->bhmd', inputs, x).reshape(b, n * prev, k)
            x = jnp.einsum('bpd,pj->bjd', z, W)
            res.append(x)
        out = jnp.sum(jnp.concatenate(res, axis=1), axis=-1)
        return out
    e = jnp.stack([tbl_0[ids[:, 0]], tbl_1[ids[:, 1]], tbl_2[ids[:, 2]], tbl_3[ids[:, 3]], tbl_4[ids[:, 4]], tbl_5[ids[:, 5]], tbl_6[ids[:, 6]], tbl_7[ids[:, 7]], tbl_8[ids[:, 8]], tbl_9[ids[:, 9]], tbl_10[ids[:, 10]], tbl_11[ids[:, 11]], tbl_12[ids[:, 12]], tbl_13[ids[:, 13]], tbl_14[ids[:, 14]], tbl_15[ids[:, 15]], tbl_16[ids[:, 16]], tbl_17[ids[:, 17]], tbl_18[ids[:, 18]], tbl_19[ids[:, 19]], tbl_20[ids[:, 20]], tbl_21[ids[:, 21]], tbl_22[ids[:, 22]], tbl_23[ids[:, 23]], tbl_24[ids[:, 24]], tbl_25[ids[:, 25]], tbl_26[ids[:, 26]], tbl_27[ids[:, 27]], tbl_28[ids[:, 28]], tbl_29[ids[:, 29]], tbl_30[ids[:, 30]], tbl_31[ids[:, 31]]], axis=1)
    z = _L0_rec_ref(e, L0_rec_W0, L0_rec_W1)
    z = z.reshape(z.shape[0], -1)
    h = jnp.concatenate([z, dense_ctx], axis=1)
    h = jnp.maximum(h @ W_top1 + b_top1, 0.0)
    h = jnp.maximum(h @ W_top2 + b_top2, 0.0)
    y = h @ W_top3
    return y

_drawn_inputs = setup_inputs


def setup_inputs(seed=0):
    import zlib

    import numpy as np

    out = dict(_drawn_inputs(seed))
    spreads = {'b_top1': (0.0, 0.1), 'b_top2': (0.0, 0.1)}
    factors = {'tbl_0': 5.001,
     'tbl_1': 4.933,
     'tbl_2': 4.979,
     'tbl_3': 5.139,
     'tbl_4': 5.186,
     'tbl_5': 4.967,
     'tbl_6': 5.068,
     'tbl_7': 5.0,
     'tbl_8': 5.08,
     'tbl_9': 5.007,
     'tbl_10': 4.504,
     'tbl_11': 5.243,
     'tbl_12': 5.213,
     'tbl_13': 4.728,
     'tbl_14': 4.902,
     'tbl_15': 5.003,
     'tbl_16': 5.232,
     'tbl_17': 4.996,
     'tbl_18': 5.367,
     'tbl_19': 5.516,
     'tbl_20': 4.609,
     'tbl_21': 4.688,
     'tbl_22': 5.22,
     'tbl_23': 4.831,
     'tbl_24': 5.094,
     'tbl_25': 5.125,
     'tbl_26': 4.712,
     'tbl_27': 4.919,
     'tbl_28': 5.306,
     'tbl_29': 5.272,
     'tbl_30': 4.82,
     'tbl_31': 4.544,
     'L0_rec_W1': 8.0}
    for name, (base, spread) in spreads.items():
        noise = np.random.default_rng([zlib.crc32(name.encode()), seed]).standard_normal(out[name].shape)
        drawn = base * np.exp(spread * noise) if base else spread * noise
        out[name] = jnp.asarray(drawn.astype(out[name].dtype))
    for name, factor in factors.items():
        out[name] = (out[name] * factor).astype(out[name].dtype)
    return out
```

```python
import concourse.bass as bass
from concourse import mybir
from contextlib import ExitStack

P = 128
F = 32
D = 32
C = 128
HALF = F // 2
ROT = HALF // 2
PAIRS = HALF * (HALF - 1) // 2
EXT = HALF + ROT
Q = P // D
BB = P // Q
UB = 8
UNITS = BB // UB
GB = 4
HJ = F // 4
H_OF_BLOCK = [0, HALF, HJ, HALF + HJ]
BANK = 512
EMB_RING = 2


def build(nc, ids, tables, W0, W1, W_top1, b_top1, W_top2, b_top2, W_top3, dense, identity, out, scratch):
    fp32, i32 = mybir.dt.float32, mybir.dt.int32
    ALU, ACT = mybir.AluOpType, mybir.ActivationFunctionType
    B = ids.shape[0]
    TILES = B // P
    NX = dense.shape[1]
    H1, H2 = W_top1.shape[1], W_top2.shape[1]
    M1, M2 = H1 // P, H2 // P

    ctx = ExitStack()
    with ctx:
        def sb(name, shape, dt=fp32):
            return ctx.enter_context(nc.sbuf_tensor(name, shape, dt))

        def sem(name):
            return ctx.enter_context(nc.semaphore(name))

        def view(handle, offset, dims, part=None):
            whole = handle[tuple(slice(None) for _ in handle.shape)] if part is None else \
                handle[(slice(*part),) + tuple(slice(None) for _ in handle.shape[1:])]
            return bass.AP(whole.tensor, whole.offset + offset, [list(whole.ap[0])] + dims)

        idx = sb("idx", [P, TILES, F], i32)
        emb = sb("emb", [P, EMB_RING, F * D])
        ET = sb("ET", [P, 2, EXT, BB])
        z = sb("z", [P, 2, UB, 2 * PAIRS])
        z2 = sb("z2", [P, 2, UB, 2 * F])
        E = sb("E", [P, 2, UB, Q * F])
        tri = sb("tri", [P, 2, F, P])
        tsg = sb("tsg", [P, 2, HJ, P])
        V = sb("V", [P, 2, F, C])
        VS = sb("VS", [P, HJ, C])
        W0g = sb("W0g", [P, HJ, C])
        w0 = sb("w0", [P, F * F // P, C])
        w1 = sb("w1", [P, F, C])
        w0T = sb("w0T", [P, F * F])
        w0sym = sb("w0sym", [P, 2, HALF, EXT])
        w0pair = sb("w0pair", [P, 2, PAIRS])
        w0x = sb("w0x", [P, 2, HALF, HALF])
        corr1 = sb("corr1", [P, HALF, C])
        corr2 = sb("corr2", [P, HALF, C])
        corrS = sb("corrS", [P, HJ, C])
        ident = sb("ident", [P, P])
        dense_in = sb("dense_in", [P, TILES, NX])
        denseT = sb("denseT", [NX, B])
        wt1 = sb("wt1", [P, 2, H1])
        wt1d = sb("wt1d", [NX, H1])
        wt2 = sb("wt2", [P, M1, H2])
        wt3 = sb("wt3", [P, M2])
        bt1 = sb("bt1", [P, M1])
        bt2 = sb("bt2", [P, M2])
        x = sb("x", [P, 2, P])
        xd = sb("xd", [NX, P])
        h1 = sb("h1", [P, M1, P])
        h2 = sb("h2", [P, M2, P])
        yrow = sb("yrow", [1, B])
        cross = tri

        def bank(name):
            return ctx.enter_context(nc.psum_tensor(name, [P, BANK], fp32))
        pair_ps = [[bank(f"pair{s}_{c}") for c in range(2)] for s in range(2)]
        sg_ps = [bank(f"sg_{c}") for c in range(2)]
        acc_ps = bank("acc")
        hid_ps = bank("hid")
        setup_ps = [pair_ps[0][0], pair_ps[0][1], pair_ps[1][0], pair_ps[1][1], sg_ps[0], sg_ps[1]]

        def sg_copy(g, part, c, col):
            return (view(tsg, g * HJ * P + col, [[1, GB * Q], [P, HJ]], (64 * part, 64 * part + 64)),
                    view(sg_ps[c], part * HJ, [[HALF, GB * Q], [1, HJ]], (64 * g, 64 * g + 64)))

        ids_loaded = sem("ids_loaded")
        w0_loaded = sem("w0_loaded")
        ident_loaded = sem("ident_loaded")
        w1_loaded = [sem(f"w1_loaded{n}") for n in range(F * C // BANK)]
        small_loaded = sem("small_loaded")
        dense_loaded = sem("dense_loaded")
        gathered = [sem(f"gathered{i}") for i in range(EMB_RING)]
        setup_mm = sem("setup_mm")
        setup_act = sem("setup_act")
        setup_dve = sem("setup_dve")
        w0sym_ready = sem("w0sym_ready")
        w0prep_ready = sem("w0prep_ready")
        corrS_zero = sem("corrS_zero")
        E_zero = sem("E_zero")
        cross_stored = [sem(f"cross_stored{s}") for s in range(2)]
        corr_loaded = [sem(f"corr_loaded{s}") for s in range(2)]
        v_half = sem("v_half")
        vs_ready = sem("vs_ready")
        et_ready = sem("et_ready")
        z_ready = sem("z_ready")
        e_ready = sem("e_ready")
        t_formed = sem("t_formed")
        t_act = sem("t_act")
        t_dve = sem("t_dve")
        acc_ready = sem("acc_ready")
        x_ready = sem("x_ready")
        h1_mm = sem("h1_mm")
        h1_ready = sem("h1_ready")
        h2_mm = sem("h2_mm")
        h2_ready = sem("h2_ready")
        y_mm = sem("y_mm")
        y_ready = sem("y_ready")
        y_stored = sem("y_stored")

        N_W0T = F * F // BANK
        N_DENSE = N_W0T
        N_CROSS = N_DENSE + 1
        WPB = BANK // C
        CROSS_BANKS = 2 * 2 * HALF // WPB
        N_MAIN = N_CROSS + CROSS_BANKS
        N_SQ = N_MAIN + 2 * F // WPB
        N_SETUP = N_SQ + HJ // WPB

        def act_banks(n):
            return n // 2 + 1

        def dve_banks(n):
            return (n + 1) // 2

        def cross_bank(s, r, w):
            return N_CROSS + (s * 2 + r) * (HALF // WPB) + w

        SMALL = 7
        CORR_DMAS = 2 * ROT + 2

        block = ctx.enter_context(nc.Block())

        @block.sync
        def _(sp):
            sp.dma_start(idx[:, :, :], ids.rearrange("(t p) f -> p t f", p=P)).then_inc(ids_loaded, 16)
            sp.dma_start(w0[:, :, :], W0.rearrange("(t p) c -> p t c", p=P)).then_inc(w0_loaded, 16)
            sp.dma_start(ident[:, :], identity).then_inc(ident_loaded, 16)
            for n in range(2 * HALF // WPB):
                sp.dma_start(w1[:, n * WPB:(n + 1) * WPB, :],
                             W1.rearrange("(h m) j -> m h j", m=C)[:, n * WPB:(n + 1) * WPB, :]).then_inc(w1_loaded[n], 16)
            for t in range(TILES):
                sp.dma_start(dense_in[:, t, :],
                             dense[t * P:(t + 1) * P, :].rearrange("(q b) n -> b q n", q=Q)).then_inc(dense_loaded, 16)
            for j, h in enumerate(H_OF_BLOCK):
                sp.dma_start(W0g[32 * j:32 * j + F, :, :],
                             W0.rearrange("(f h) c -> f h c", h=F)[:, h:h + HJ, :]).then_inc(small_loaded, 16)
            sp.dma_start(wt1[:, :, :], W_top1[0:2 * C, :].rearrange("(k p) n -> p k n", p=P)).then_inc(small_loaded, 16)
            sp.dma_start(wt1d[:, :], W_top1[2 * C:2 * C + NX, :]).then_inc(small_loaded, 16)
            sp.dma_start(wt2[:, :, :], W_top2.rearrange("(k p) n -> p k n", p=P)).then_inc(small_loaded, 16)
            sp.dma_start(wt3[:, :], W_top3).then_inc(small_loaded, 16)
            sp.dma_start(bt1[:, :], b_top1).then_inc(small_loaded, 16)
            sp.dma_start(bt2[:, :], b_top2).then_inc(small_loaded, 16)
            for s in range(2):
                for r in range(2):
                    sp.wait_ge(setup_act, act_banks(cross_bank(s, r, HALF // WPB - 1)))
                    sp.wait_ge(setup_dve, dve_banks(cross_bank(s, r, HALF // WPB - 1)))
                    rows = scratch[s][r * ROT:(r + 1) * ROT, :, :, :].rearrange("o t w j -> (o t) w j")
                    src = view(cross, (s * 2 + r) * HALF * C, [[C, HALF], [1, C]])
                    sp.dma_start(rows[:, 0:HALF, :], src).then_inc(cross_stored[s], 16)
                    sp.dma_start(rows[:, HALF:EXT, :], view(cross, (s * 2 + r) * HALF * C, [[C, ROT], [1, C]]))\
                      .then_inc(cross_stored[s], 16)
                    if r == 0:
                        again = scratch[s][HALF:EXT, :, :, :].rearrange("o t w j -> (o t) w j")
                        sp.dma_start(again[:, 0:HALF, :], src).then_inc(cross_stored[s], 16)
            so, st, sw = HALF * EXT * C, EXT * C, C
            for s in range(2):
                sp.wait_ge(cross_stored[s], 16 * 5)
                if s == 0:
                    sp.wait_ge(corrS_zero, 1)
                else:
                    sp.wait_ge(v_half, 2)
                whole = scratch[s][:, :, :, :]
                for k in range(1, ROT + 1):
                    n = HALF if k < ROT else ROT
                    part = (k - 1) * HALF
                    for dst, off in ((corr1, k * so), (corr2, k * sw)):
                        sp.dma_start(dst[part:part + n, :, :],
                                     bass.AP(whole.tensor, off, [[so + sw, n], [st, HALF], [1, C]]))\
                          .then_inc(corr_loaded[s], 16)
                for jj in range(2):
                    j = 2 * jj + 1 - s
                    sp.dma_start(corrS[32 * j + s * HALF:32 * j + s * HALF + HALF, :, :],
                                 bass.AP(whole.tensor, jj * HJ * st, [[so + sw, HALF], [st, HJ], [1, C]]))\
                      .then_inc(corr_loaded[s], 16)
            sp.wait_ge(y_ready, TILES)
            sp.dma_start(out.rearrange("b o -> o b"), yrow[0:1, :]).then_inc(y_stored, 16)
            sp.wait_ge(y_stored, 16)

        @block.gpsimd
        def _(pool):
            pool.wait_ge(ids_loaded, 16)
            for t in range(TILES):
                if t >= EMB_RING:
                    pool.wait_ge(et_ready, t - EMB_RING + 1)
                for f in range(F):
                    pool.indirect_dma_start(
                        out=emb[:, t % EMB_RING, f * D:(f + 1) * D], out_offset=None, in_=tables[f][:, :],
                        in_offset=bass.IndirectOffsetOnAxis(ap=idx[:, t, f:f + 1], axis=0),
                    ).then_inc(gathered[t % EMB_RING], 16)

        @block.scalar
        def _(act):
            def setup_copy(n, dst, rows=P):
                act.wait_ge(setup_mm, n + 1)
                nc.scalar.copy(dst, setup_ps[n % 6][0:rows, :]).then_inc(setup_act, 1)

            def spread(u, ring, count):
                for q in range(Q):
                    lo, hi = q * D, (q + 1) * D
                    nc.scalar.copy(view(E, ring * UB * Q * F + q * F, [[Q * F, UB], [HALF, 2], [1, HALF]], (lo, hi)),
                                   view(ET, u * UB, [[1, UB], [EXT * BB, 2], [BB, HALF]], (lo, hi)))
                nc.scalar.copy(view(z2, ring * UB * 2 * F + F, [[2 * F, UB], [HALF, 2], [1, HALF]]),
                               view(ET, u * UB, [[1, UB], [EXT * BB, 2], [BB, HALF]])).then_inc(e_ready, 1)

            def empty(u, c, group):
                col = (u * UB + c * GB) * Q
                act.wait_ge(t_formed, group)
                for part in range(2):
                    nc.scalar.copy(*sg_copy(0, part, c, col))
                nc.scalar.copy(view(tri, col, [[1, GB * Q], [P, F]], (0, PAIRS)),
                               view(pair_ps[0][c], 0, [[F, GB * Q], [1, F]], (0, PAIRS))).then_inc(t_act, 1)

            def mlp_input(t):
                act.wait_ge(acc_ready, t + 1)
                nc.scalar.copy(xd[:, :], denseT[:, bass.ts(t, P)])
                nc.scalar.copy(x[:, :, :], acc_ps[:, 0:2 * P].rearrange("p (k b) -> p k b", k=2)).then_inc(x_ready, 1)

            def mlp_hidden1(t):
                act.wait_ge(h1_mm, t + 1)
                for m in range(M1):
                    last = nc.scalar.activation(h1[:, m, :], hid_ps[:, m * P:(m + 1) * P], ACT.Relu, bias=bt1[:, m:m + 1])
                last.then_inc(h1_ready, 1)

            def mlp_hidden2(t):
                act.wait_ge(h2_mm, t + 1)
                for m in range(M2):
                    last = nc.scalar.activation(h2[:, m, :], hid_ps[:, m * P:(m + 1) * P], ACT.Relu, bias=bt2[:, m:m + 1])
                last.then_inc(h2_ready, 1)

            def mlp_output(t):
                act.wait_ge(y_mm, t + 1)
                nc.scalar.copy(yrow[0:1, bass.ts(t, P)].rearrange("o (q b) -> o b q", q=Q),
                               hid_ps[0:1, 0:P].rearrange("o (b q) -> o b q", q=Q)).then_inc(y_ready, 1)

            def tile(t, first):
                act.wait_ge(et_ready, t + 1)
                for u in range(UNITS):
                    if not (first and u < 2):
                        act.wait_ge(t_formed, 2 * (t * UNITS + u) - 2)
                    spread(u, u % 2, None)
                    if not first:
                        if u == 1:
                            mlp_input(t - 1)
                        if u == 3:
                            mlp_hidden1(t - 1)
                    if u >= 1:
                        for c in range(2):
                            empty(u - 1, c, 2 * (t * UNITS + u - 1) + c + 1)
                for c in range(2):
                    empty(UNITS - 1, c, 2 * (t * UNITS + UNITS - 1) + c + 1)
                if not first:
                    mlp_hidden2(t - 1)
                    mlp_output(t - 1)

            setup_copy(0, w0T[:, 0:BANK])
            setup_copy(N_DENSE, denseT[:, :], NX)
            for n in range(N_CROSS, N_MAIN):
                if n % 2 == 0:
                    setup_copy(n, view(cross, (n - N_CROSS) * BANK, [[1, BANK]]))
            for n in range(N_MAIN, N_SQ):
                if n % 2 == 0:
                    setup_copy(n, view(V, (n - N_MAIN) * BANK, [[1, BANK]], (0, PAIRS)), PAIRS)
            for n in range(N_SQ, N_SETUP):
                if n % 2 == 0:
                    setup_copy(n, view(VS, (n - N_SQ) * BANK, [[1, BANK]]))
            act.wait_ge(E_zero, 1)
            for s in range(2):
                act.wait_ge(cross_stored[s], 16 * 5)
            act.wait_ge(small_loaded, 16 * (SMALL + 3))
            tile(0, True)
            with act.Fori(1, TILES) as t:
                tile(t, False)
            mlp_input(TILES - 1)
            mlp_hidden1(TILES - 1)
            mlp_hidden2(TILES - 1)
            mlp_output(TILES - 1)

        @block.vector
        def _(dve):
            def setup_copy(n, dst, rows=P):
                dve.wait_ge(setup_mm, n + 1)
                nc.vector.tensor_copy(dst, setup_ps[n % 6][0:rows, :]).then_inc(setup_dve, 1)

            def add_corrections(s):
                own = V[0:PAIRS, s, (1 - s) * HALF:(2 - s) * HALF, :]
                dve.wait_ge(corr_loaded[s], 16 * CORR_DMAS)
                for n, corr in enumerate((corr1, corr2)):
                    nc.vector.tensor_tensor(own, own, corr[0:PAIRS, :, :], ALU.add).then_inc(v_half, 1)
                    dve.wait_ge(v_half, 2 * s + n + 1)

            def transpose_tile(t, slot, gathers):
                dve.wait_ge(gathered[slot], gathers)
                for s in range(2):
                    nc.vector.transpose(view(ET, s * EXT * BB, [[1, HALF * BB]]), emb[:, slot, s * HALF * D:(s + 1) * HALF * D])
                    last = nc.vector.transpose(view(ET, (s * EXT + HALF) * BB, [[1, ROT * BB]]),
                                               emb[:, slot, s * HALF * D:(s * HALF + ROT) * D])
                last.then_inc(et_ready, 1)
                dve.wait_ge(et_ready, t + 1)

            def products(u, ring):
                o = u * UB
                for s in range(2):
                    nc.vector.tensor_tensor(
                        view(z, ring * UB * 2 * PAIRS + s * PAIRS, [[2 * PAIRS, UB], [HALF, ROT - 1], [1, HALF]]),
                        view(ET, s * EXT * BB + o, [[1, UB], [0, ROT - 1], [BB, HALF]]),
                        view(ET, s * EXT * BB + BB + o, [[1, UB], [BB, ROT - 1], [BB, HALF]]), ALU.mult)
                nc.vector.tensor_tensor(
                    view(z, ring * UB * 2 * PAIRS + HALF * (ROT - 1), [[2 * PAIRS, UB], [PAIRS, 2], [1, ROT]]),
                    view(ET, o, [[1, UB], [EXT * BB, 2], [BB, ROT]]),
                    view(ET, ROT * BB + o, [[1, UB], [EXT * BB, 2], [BB, ROT]]), ALU.mult)
                e = view(ET, o, [[1, UB], [EXT * BB, 2], [BB, HALF]])
                nc.vector.tensor_tensor(view(z2, ring * UB * 2 * F, [[2 * F, UB], [HALF, 2], [1, HALF]]),
                                        e, e, ALU.mult).then_inc(z_ready, 1)

            def empty(u, c, group):
                col = (u * UB + c * GB) * Q
                dve.wait_ge(t_formed, group)
                for part in range(2):
                    nc.vector.tensor_copy(*sg_copy(1, part, c, col))
                nc.vector.tensor_copy(view(tri, F * P + col, [[1, GB * Q], [P, F]], (0, PAIRS)),
                                      view(pair_ps[1][c], 0, [[F, GB * Q], [1, F]], (0, PAIRS))).then_inc(t_dve, 1)

            def tile(t, slot, gathers, first):
                if not first:
                    dve.wait_ge(e_ready, t * UNITS)
                transpose_tile(t, slot, gathers)
                for u in range(UNITS):
                    if not (first and u < 2):
                        dve.wait_ge(t_formed, 2 * (t * UNITS + u) - 2)
                    products(u, u % 2)
                    if first and u == 3:
                        add_corrections(0)
                    if u >= 1:
                        for c in range(2):
                            empty(u - 1, c, 2 * (t * UNITS + u - 1) + c + 1)
                for c in range(2):
                    empty(UNITS - 1, c, 2 * (t * UNITS + UNITS - 1) + c + 1)

            nc.vector.memset(E[:, :, :, :], 0.0).then_inc(E_zero, 1)
            nc.vector.memset(corrS[:, :, :], 0.0).then_inc(corrS_zero, 1)
            setup_copy(1, w0T[:, BANK:2 * BANK])
            dve.wait_ge(setup_act, 1)
            dve.wait_ge(setup_dve, 1)
            for s in range(2):
                o = s * HALF * (F + 1)
                nc.vector.tensor_tensor(w0x[:, s, :, :],
                                        view(w0T, s * HALF * F + (1 - s) * HALF, [[F, HALF], [1, HALF]]),
                                        view(w0T, (1 - s) * HALF * F + s * HALF, [[1, HALF], [F, HALF]]), ALU.add)
                for q0, q1 in ((0, HALF), (HALF, EXT)):
                    n = q1 - q0
                    last = nc.vector.tensor_tensor(w0sym[:, s, :, q0:q1], view(w0T, o, [[F, HALF], [1, n]]),
                                                   view(w0T, o, [[1, HALF], [F, n]]), ALU.add)
            last.then_inc(w0sym_ready, 1)
            dve.wait_ge(w0sym_ready, 1)
            for s in range(2):
                nc.vector.tensor_copy(view(w0pair, s * PAIRS, [[HALF, ROT - 1], [1, HALF]]),
                                      view(w0sym, s * HALF * EXT + 1, [[1, ROT - 1], [EXT + 1, HALF]]))
                last = nc.vector.tensor_copy(view(w0pair, s * PAIRS + HALF * (ROT - 1), [[1, ROT]]),
                                             view(w0sym, s * HALF * EXT + ROT, [[EXT + 1, ROT]]))
            last.then_inc(w0prep_ready, 1)
            for n in range(N_CROSS, N_MAIN):
                if n % 2 == 1:
                    setup_copy(n, view(cross, (n - N_CROSS) * BANK, [[1, BANK]]))
            for n in range(N_MAIN, N_SQ):
                if n % 2 == 1:
                    setup_copy(n, view(V, (n - N_MAIN) * BANK, [[1, BANK]], (0, PAIRS)), PAIRS)
            for n in range(N_SQ, N_SETUP):
                if n % 2 == 1:
                    setup_copy(n, view(VS, (n - N_SQ) * BANK, [[1, BANK]]))
            dve.wait_ge(setup_act, act_banks(N_SETUP - 1))
            dve.wait_ge(setup_dve, dve_banks(N_SETUP - 1))
            for s in range(2):
                dve.wait_ge(cross_stored[s], 16 * 5)
            tile(0, 0, 16 * F, True)
            add_corrections(1)
            nc.vector.tensor_tensor(VS[:, :, :], VS[:, :, :], corrS[:, :, :], ALU.add).then_inc(vs_ready, 1)
            tile(1, 1, 16 * F, False)
            with dve.Fori(1, TILES // EMB_RING) as i:
                for slot in range(EMB_RING):
                    tile(i * EMB_RING + slot, slot, (i + 1) * (16 * F), False)

        @block.tensor
        def _(pe):
            def setup_bank(n):
                if n >= 6:
                    if n % 2 == 0:
                        pe.wait_ge(setup_act, act_banks(n - 6))
                    else:
                        pe.wait_ge(setup_dve, dve_banks(n - 6))
                return setup_ps[n % 6]

            def form(u, t, first):
                ring = u % 2
                pe.wait_ge(z_ready, t * UNITS + u + 1)
                pe.wait_ge(e_ready, t * UNITS + u + 1)
                for c in range(2):
                    if not (first and u == 0):
                        pe.wait_ge(t_act, 2 * (t * UNITS + u) + c - 1)
                        pe.wait_ge(t_dve, 2 * (t * UNITS + u) + c - 1)
                    for b in range(GB):
                        bb = c * GB + b
                        for s in range(2):
                            nc.tensor.matmul(pair_ps[s][c][0:PAIRS, b * Q * F:(b + 1) * Q * F],
                                             z[:, ring, bb, s * PAIRS:(s + 1) * PAIRS], E[:, ring, bb, :],
                                             start=True, stop=True)
                    for b in range(GB):
                        bb = c * GB + b
                        for g in range(2):
                            for half in range(2):
                                row = 32 * (2 * g + half)
                                last = nc.tensor.matmul(
                                    sg_ps[c][row:row + F, b * Q * HALF:(b + 1) * Q * HALF], z2[:, ring, bb, g * F:(g + 1) * F],
                                    view(E, (ring * UB + bb) * Q * F + half * HALF, [[F, Q], [1, HALF]]),
                                    start=True, stop=True)
                    last.then_inc(t_formed, 1)

            def contract(t, wait_v, between):
                pe.wait_ge(t_act, 2 * UNITS * (t + 1))
                pe.wait_ge(t_dve, 2 * UNITS * (t + 1))
                if wait_v:
                    pe.wait_ge(v_half, 2)
                for s in range(2):
                    if wait_v and s == 1:
                        pe.wait_ge(v_half, 4)
                    for h in range(F):
                        nc.tensor.matmul(acc_ps[:, P:2 * P], V[0:PAIRS, s, h, :], tri[0:PAIRS, s, h, :],
                                         start=(s == 0 and h == 0), stop=False)
                    if s == 0 and between:
                        between()
                if wait_v:
                    pe.wait_ge(vs_ready, 1)
                for h in range(HJ):
                    nc.tensor.matmul(acc_ps[:, P:2 * P], VS[:, h, :], tsg[:, 0, h, :], start=False, stop=(h == HJ - 1))
                for h in range(HJ):
                    last = nc.tensor.matmul(acc_ps[:, 0:P], W0g[:, h, :], tsg[:, 1, h, :], start=(h == 0), stop=(h == HJ - 1))
                last.then_inc(acc_ready, 1)

            def mlp1(t):
                pe.wait_ge(x_ready, t + 1)
                for m in range(M1):
                    o = hid_ps[:, m * P:(m + 1) * P]
                    for k in range(2):
                        nc.tensor.matmul(o, wt1[:, k, m * P:(m + 1) * P], x[:, k, :], start=(k == 0), stop=False)
                    last = nc.tensor.matmul(o, wt1d[:, m * P:(m + 1) * P], xd[:, :], start=False, stop=True)
                last.then_inc(h1_mm, 1)

            def mlp2(t):
                pe.wait_ge(h1_ready, t + 1)
                for m in range(M2):
                    for k in range(M1):
                        last = nc.tensor.matmul(hid_ps[:, m * P:(m + 1) * P], wt2[:, k, m * P:(m + 1) * P],
                                                h1[:, k, :], start=(k == 0), stop=(k == M1 - 1))
                last.then_inc(h2_mm, 1)

            def mlp3(t):
                pe.wait_ge(h2_ready, t + 1)
                for k in range(M2):
                    last = nc.tensor.matmul(hid_ps[0:1, 0:P], wt3[:, k:k + 1], h2[:, k, :], start=(k == 0), stop=(k == M2 - 1))
                last.then_inc(y_mm, 1)

            pe.wait_ge(ident_loaded, 16)
            pe.wait_ge(w0_loaded, 16)
            for n in range(N_W0T):
                for i in range(BANK // P):
                    last = nc.tensor.transpose(setup_ps[n][:, i * P:(i + 1) * P], w0[:, n * (BANK // P) + i, :], ident[:, :])
                last.then_inc(setup_mm, 1)
            pe.wait_ge(dense_loaded, 16 * TILES)
            for t in range(TILES):
                last = nc.tensor.transpose(setup_ps[N_DENSE][0:NX, t * P:(t + 1) * P], dense_in[:, t, :], ident[:, :])
            last.then_inc(setup_mm, 1)
            pe.wait_ge(w0prep_ready, 1)
            for s in range(2):
                for r in range(2):
                    for w in range(HALF // WPB):
                        n = cross_bank(s, r, w)
                        if r == 0:
                            pe.wait_ge(w1_loaded[s * (HALF // WPB) + w], 16)
                        nc.tensor.matmul(setup_bank(n)[:, :], w0x[:, s, r * ROT:(r + 1) * ROT, :].rearrange("m o t -> m (o t)"),
                                         w1[:, s * HALF + w * WPB:s * HALF + (w + 1) * WPB, :].rearrange("m w j -> m (w j)"),
                                         start=True, stop=True).then_inc(setup_mm, 1)
            for s in range(2):
                for h in range(F // WPB):
                    n = N_MAIN + s * (F // WPB) + h
                    nc.tensor.matmul(setup_bank(n)[0:PAIRS, :], w0pair[:, s, :],
                                     w1[:, h * WPB:(h + 1) * WPB, :].rearrange("m w j -> m (w j)"),
                                     start=True, stop=True).then_inc(setup_mm, 1)
            for i in range(HJ // WPB):
                ps = setup_bank(N_SQ + i)
                for j in range(4):
                    h = H_OF_BLOCK[j] + i * WPB
                    last = nc.tensor.matmul(ps[32 * j:32 * j + F, :], w0T[:, 0:F * F:F + 1],
                                            w1[:, h:h + WPB, :].rearrange("m w j -> m (w j)"), start=True, stop=True)
                last.then_inc(setup_mm, 1)
            pe.wait_ge(setup_act, act_banks(N_SETUP - 1))
            pe.wait_ge(setup_dve, dve_banks(N_SETUP - 1))
            pe.wait_ge(small_loaded, 16 * (SMALL + 3))

            for u in range(UNITS):
                form(u, 0, True)
            contract(0, True, None)
            with pe.Fori(1, TILES) as t:
                form(0, t, False)
                form(1, t, False)
                mlp1(t - 1)
                form(2, t, False)
                form(3, t, False)
                mlp2(t - 1)
                contract(t, False, lambda: mlp3(t - 1))
            mlp1(TILES - 1)
            mlp2(TILES - 1)
            mlp3(TILES - 1)


def kernel(**inputs):
    import numpy as np
    import concourse.bacc as bacc
    from concourse.bass_utils import run_bass_kernel_spmd

    nc = bacc.Bacc("TRN2", target_bir_lowering=False, num_devices=1)
    arrays = {}

    def given(name, array):
        array = np.ascontiguousarray(array)
        arrays[name] = array
        return nc.dram_tensor(name, array.shape, mybir.dt.from_np(array.dtype), kind="ExternalInput").ap()

    ids = given("ids_in", inputs["ids"])
    tables = [given(f"tbl_{f}_in", inputs[f"tbl_{f}"]) for f in range(F)]
    by_partition = {name: np.asarray(inputs[name]).reshape(-1, P).T for name in ("b_top1", "b_top2", "W_top3")}
    args = [given(name + "_in", by_partition.get(name, inputs[name])) for name in
            ("L0_rec_W0", "L0_rec_W1", "W_top1", "b_top1", "W_top2", "b_top2", "W_top3", "dense_ctx")]
    identity = given("identity_in", np.eye(P, dtype=np.float32))
    out = nc.dram_tensor("out_y", (ids.shape[0], 1), mybir.dt.float32, kind="ExternalOutput").ap()
    scratch = [nc.dram_tensor(f"cross_scratch{s}", (EXT, HALF, EXT, C), mybir.dt.float32, kind="Internal").ap()
               for s in range(2)]
    build(nc, ids, tables, *args, identity, out, scratch)
    result = run_bass_kernel_spmd(nc, [arrays], core_ids=[0])
    return result.results[0]["out_y"]
```

```python
import concourse.bass as bass
from concourse import mybir
from contextlib import ExitStack

P = 128
F = 32
D = 32
C = 128
HALF = F // 2
PAIRS = HALF * (HALF - 1) // 2
QTR = F // 4
ROT = QTR // 2
EXT = QTR + ROT
QPAIRS = QTR * (QTR - 1) // 2
OWN = 64
Q = P // D
BB = P // Q
UB = 8
UNITS = BB // UB
GB = 4
QUARTER_OF_BLOCK = [0, 2, 1, 3]
BANK = 512
EMB_RING = 2


def build(nc, ids, tables, W0, W1, W_top1, b_top1, W_top2, b_top2, W_top3, dense, identity, out, scratch, scratch_q):
    fp32, i32 = mybir.dt.float32, mybir.dt.int32
    ALU, ACT = mybir.AluOpType, mybir.ActivationFunctionType
    B = ids.shape[0]
    TILES = B // P
    NX = dense.shape[1]
    H1, H2 = W_top1.shape[1], W_top2.shape[1]
    M1, M2 = H1 // P, H2 // P

    ctx = ExitStack()
    with ctx:
        def sb(name, shape, dt=fp32):
            return ctx.enter_context(nc.sbuf_tensor(name, shape, dt))

        def sem(name):
            return ctx.enter_context(nc.semaphore(name))

        def view(handle, offset, dims, part=None):
            whole = handle[tuple(slice(None) for _ in handle.shape)] if part is None else \
                handle[(slice(*part),) + tuple(slice(None) for _ in handle.shape[1:])]
            return bass.AP(whole.tensor, whole.offset + offset, [list(whole.ap[0])] + dims)

        idx = sb("idx", [P, TILES, F], i32)
        emb = sb("emb", [P, EMB_RING, F * D])
        ET = sb("ET", [P, 4, EXT, BB])
        z = sb("z", [P, 2, UB, 2 * PAIRS])
        z2 = sb("z2", [P, 2, UB, 2 * F])
        E = sb("E", [P, 2, UB, Q * F])
        T = sb("T", [P, 4 * HALF * P])
        TX, TOWN, TSG = 0, 2 * HALF * P, 3 * HALF * P
        VX = sb("VX", [P, 2, HALF, C])
        VO = sb("VO", [P, HALF, C])
        VS = sb("VS", [P, QTR, C])
        W0g = sb("W0g", [P, QTR, C])
        w1 = sb("w1", [P, F, C])
        w0T = sb("w0T", [P, F * F])
        w0x = sb("w0x", [P, 2, HALF, HALF])
        w0xq = sb("w0xq", [P, 2, 2, QTR, QTR])
        w0sym = sb("w0sym", [P, 4, QTR, EXT])
        w0pair = sb("w0pair", [P, 2, PAIRS])
        w0own = sb("w0own", [P, 2, OWN])
        corrX = sb("corrX", [P, 2, 2, HALF, C])
        corrO = sb("corrO", [P, 2, HALF, C])
        corrS = sb("corrS", [P, QTR, C])
        ident = sb("ident", [P, P])
        dense_in = sb("dense_in", [P, TILES, NX])
        denseT = sb("denseT", [NX, B])
        wt3 = sb("wt3", [P, M2])
        bt1 = sb("bt1", [P, M1])
        bt2 = sb("bt2", [P, M2])
        x = sb("x", [P, 2, P])
        xd = sb("xd", [NX, P])
        yrow = sb("yrow", [1, B])
        w0 = view(corrX, 0, [[C, F * F // P], [1, C]])
        mlp_room = [0, 2 * M1, 3 * M1, 3 * M1 + M1 * M2, 4 * M1 + M1 * M2, 4 * M1 + M1 * M2 + M2]
        wt1, wt1d, wt2, h1, h2 = (w1[:, lo:hi, :] for lo, hi in zip(mlp_room, mlp_room[1:]))
        wt1 = wt1.rearrange("p (k m) c -> p k (m c)", k=2)
        wt1d = wt1d[0:NX, :, :].rearrange("p m c -> p (m c)")
        wt2 = wt2.rearrange("p (k m) c -> p k (m c)", k=M1)
        cross = T
        cross_q = view(corrX, 2 * HALF * C, [[1, 2 * QTR * C]])

        def bank(name):
            return ctx.enter_context(nc.psum_tensor(name, [P, BANK], fp32))
        pair_ps = [[bank(f"pair{s}_{c}") for c in range(2)] for s in range(2)]
        sg_ps = [bank(f"sg_{c}") for c in range(2)]
        acc_ps = bank("acc")
        hid_ps = bank("hid")
        setup_ps = [pair_ps[0][0], pair_ps[0][1], pair_ps[1][0], pair_ps[1][1], sg_ps[0], sg_ps[1]]

        def x_copy(s, c, col):
            return (view(T, TX + s * HALF * P + col, [[1, GB * Q], [P, HALF]], (0, PAIRS)),
                    view(pair_ps[s][c], (1 - s) * HALF, [[F, GB * Q], [1, HALF]], (0, PAIRS)))

        def own_copy(s, c, col):
            return (view(T, TOWN + col, [[1, GB * Q], [P, HALF]], (s * OWN, (s + 1) * OWN)),
                    view(pair_ps[s][c], s * HALF, [[F, GB * Q], [1, HALF]], (0, OWN)))

        def sg_copy(g, part, c, col):
            return (view(T, TSG + g * QTR * P + col, [[1, GB * Q], [P, QTR]], (64 * part, 64 * part + 64)),
                    view(sg_ps[c], part * QTR, [[HALF, GB * Q], [1, QTR]], (64 * g, 64 * g + 64)))

        ids_loaded = sem("ids_loaded")
        w0_loaded = sem("w0_loaded")
        ident_loaded = sem("ident_loaded")
        w1_loaded = [sem(f"w1_loaded{n}") for n in range(F * C // BANK)]
        dense_loaded = sem("dense_loaded")
        w0g_loaded = sem("w0g_loaded")
        mlp_loaded = sem("mlp_loaded")
        gathered = [sem(f"gathered{i}") for i in range(EMB_RING)]
        setup_mm = sem("setup_mm")
        setup_act = sem("setup_act")
        setup_dve = sem("setup_dve")
        w0x_ready = sem("w0x_ready")
        w0sym_ready = sem("w0sym_ready")
        w0pair_ready = sem("w0pair_ready")
        corrO_zero = sem("corrO_zero")
        corrS_zero = sem("corrS_zero")
        w0own_zero = sem("w0own_zero")
        w0own_ready = sem("w0own_ready")
        E_zero = sem("E_zero")
        quarters_stored = [sem(f"quarters_stored{s}") for s in range(2)]
        half_stored = [sem(f"half_stored{s}") for s in range(2)]
        corrX_loaded = [sem(f"corrX_loaded{s}") for s in range(2)]
        corrO_loaded = sem("corrO_loaded")
        v_x = sem("v_x")
        v_own = sem("v_own")
        v_squares = sem("v_squares")
        et_ready = sem("et_ready")
        z_ready = sem("z_ready")
        e_ready = sem("e_ready")
        t_formed = sem("t_formed")
        t_act = sem("t_act")
        t_dve = sem("t_dve")
        acc_ready = sem("acc_ready")
        x_ready = sem("x_ready")
        h1_mm = sem("h1_mm")
        h1_ready = sem("h1_ready")
        h2_mm = sem("h2_mm")
        h2_ready = sem("h2_ready")
        y_mm = sem("y_mm")
        y_ready = sem("y_ready")
        y_stored = sem("y_stored")

        WPB = BANK // C
        N_W0T = F * F // BANK
        N_DENSE = N_W0T
        N_CROSS = N_DENSE + 1
        QUARTER_BANKS = QTR // WPB
        CROSS_BANKS = QUARTER_BANKS + 2 * HALF // WPB
        N_OWN = N_CROSS + 2 * CROSS_BANKS
        N_X = N_OWN + HALF // WPB
        N_SQ = N_X + 2 * HALF // WPB
        N_SETUP = N_SQ + QTR // WPB

        def act_banks(n):
            return n if n > 1 else n + 1

        def quarter_bank(s, w):
            return N_CROSS + s * CROSS_BANKS + w

        def cross_bank(s, r, w):
            return N_CROSS + s * CROSS_BANKS + QUARTER_BANKS + r * (HALF // WPB) + w

        MLP_LOADS = 6
        STORES_QUARTER, STORES_HALF = 3, 8
        LOADS_QUARTER, LOADS_HALF = 5, 14

        block = ctx.enter_context(nc.Block())

        @block.sync
        def _(sp):
            sp.dma_start(idx[:, :, :], ids.rearrange("(t p) f -> p t f", p=P)).then_inc(ids_loaded, 16)
            sp.dma_start(w0[:, :, :], W0.rearrange("(t p) c -> p t c", p=P)).then_inc(w0_loaded, 16)
            sp.dma_start(ident[:, :], identity).then_inc(ident_loaded, 16)
            for n in range(F // WPB):
                sp.dma_start(w1[:, n * WPB:(n + 1) * WPB, :],
                             W1.rearrange("(h m) j -> m h j", m=C)[:, n * WPB:(n + 1) * WPB, :]).then_inc(w1_loaded[n], 16)
            for t in range(TILES):
                sp.dma_start(dense_in[:, t, :],
                             dense[t * P:(t + 1) * P, :].rearrange("(q b) n -> b q n", q=Q)).then_inc(dense_loaded, 16)
            for j, quarter in enumerate(QUARTER_OF_BLOCK):
                sp.dma_start(W0g[32 * j:32 * j + F, :, :],
                             W0.rearrange("(f h) c -> f h c", h=F)[:, quarter * QTR:(quarter + 1) * QTR, :])\
                  .then_inc(w0g_loaded, 16)

            def store(dst, src, stored):
                sp.dma_start(dst.rearrange("w o t j -> (o t) w j"), src).then_inc(stored, 16)

            def store_quarters(s):
                sp.wait_ge(setup_act, act_banks(quarter_bank(s, QUARTER_BANKS - 1)))
                for u in range(2):
                    cells, done = scratch_q[2 * s + u], quarters_stored[s]
                    src = cross_q[u * 64:(u + 1) * 64, s * QTR * C:(s + 1) * QTR * C].rearrange("p (w j) -> p w j", j=C)
                    store(cells[0:QTR, 0:QTR, :, :], src, done)
                    store(cells[QTR:EXT, 0:QTR, :, :], src[:, 0:ROT, :], done)
                    store(cells[0:QTR, QTR:EXT, :, :], src[0:ROT * QTR, :, :], done)

            def store_half(s):
                for r in range(2):
                    sp.wait_ge(setup_act, act_banks(cross_bank(s, r, HALF // WPB - 1)))
                    cells, done = scratch[s], half_stored[s]
                    src = cross[:, (s * 2 + r) * HALF * C:(s * 2 + r + 1) * HALF * C].rearrange("p (w j) -> p w j", j=C)
                    o = r * EXT
                    for u in range(2):
                        store(cells[u * EXT:u * EXT + QTR, o:o + QTR, :, :], src[:, u * QTR:(u + 1) * QTR, :], done)
                    own = src[:, r * QTR:(r + 1) * QTR, :]
                    store(cells[o + QTR:o + EXT, o:o + QTR, :, :], own[:, 0:ROT, :], done)
                    store(cells[o:o + QTR, o + QTR:o + EXT, :, :], own[0:ROT * HALF, :, :], done)

            def load_rotations(dst, row, cells, off, so, sw, width, loaded):
                for which, step in ((0, so), (1, sw)):
                    for k0, k1, n in ((1, ROT, QTR), (ROT, ROT + 1, ROT)):
                        r0 = row + (k0 - 1) * QTR
                        sp.dma_start(dst[r0:r0 + (k1 - k0) * n, which, :, :].rearrange("r t j -> r (t j)"),
                                     bass.AP(cells.tensor, off + k0 * step, [[step, k1 - k0], [so + sw, n], [1, width]]))\
                          .then_inc(loaded, 16)

            def load_quarter(g):
                so, sw = QTR * C, EXT * QTR * C
                cells = scratch_q[g][:, :, :, :]
                other = (1 - g % 2) * QTR
                load_rotations(corrO[:, :, other:other + QTR, :], g // 2 * OWN + g % 2 * QPAIRS, cells, 0, so, sw, QTR * C,
                               corrO_loaded)
                row = 32 * QUARTER_OF_BLOCK[g + 1 - 2 * (g % 2)] + g * QTR
                sp.dma_start(corrS[row:row + QTR, :, :].rearrange("r t j -> r (t j)"),
                             bass.AP(cells.tensor, 0, [[so + sw, QTR], [1, QTR * C]])).then_inc(corrO_loaded, 16)

            def load_half(s):
                so, sw = HALF * C, 2 * EXT * HALF * C
                cells = scratch[s][:, :, :, :]
                for u in range(2):
                    load_rotations(corrX[:, s, :, :, :], u * QPAIRS, cells, u * EXT * (so + sw), so, sw, HALF * C,
                                   corrX_loaded[s])
                for which, step_p, step_q in ((0, sw, so), (1, so, sw)):
                    sp.dma_start(corrX[2 * QPAIRS:PAIRS, s, which, :, :].rearrange("r t j -> r (t j)"),
                                 bass.AP(cells.tensor, EXT * step_q, [[step_p, QTR], [step_q, QTR], [1, HALF * C]]))\
                      .then_inc(corrX_loaded[s], 16)
                for v in range(2):
                    row = 32 * QUARTER_OF_BLOCK[2 * (1 - s) + v] + s * HALF
                    for u in range(2):
                        sp.dma_start(corrS[row + u * QTR:row + (u + 1) * QTR, :, :].rearrange("r t j -> r (t j)"),
                                     bass.AP(cells.tensor, u * EXT * (so + sw) + v * QTR * C, [[so + sw, QTR], [1, QTR * C]]))\
                          .then_inc(corrX_loaded[s], 16)

            store_quarters(0)
            store_half(0)
            sp.wait_ge(corrO_zero, 1)
            sp.wait_ge(corrS_zero, 1)
            sp.wait_ge(quarters_stored[0], 16 * 2 * STORES_QUARTER)
            load_quarter(0)
            load_quarter(1)
            store_quarters(1)
            store_half(1)
            sp.wait_ge(half_stored[0], 16 * STORES_HALF)
            load_half(0)
            sp.wait_ge(quarters_stored[1], 16 * 2 * STORES_QUARTER)
            load_quarter(2)
            load_quarter(3)
            sp.wait_ge(half_stored[1], 16 * STORES_HALF)
            load_half(1)
            sp.wait_ge(setup_mm, N_SETUP)
            sp.dma_start(wt1[:, :, :], W_top1[0:2 * C, :].rearrange("(k p) n -> p k n", p=P)).then_inc(mlp_loaded, 16)
            sp.dma_start(wt1d[:, :], W_top1[2 * C:2 * C + NX, :]).then_inc(mlp_loaded, 16)
            sp.dma_start(wt2[:, :, :], W_top2.rearrange("(k p) n -> p k n", p=P)).then_inc(mlp_loaded, 16)
            sp.dma_start(wt3[:, :], W_top3).then_inc(mlp_loaded, 16)
            sp.dma_start(bt1[:, :], b_top1).then_inc(mlp_loaded, 16)
            sp.dma_start(bt2[:, :], b_top2).then_inc(mlp_loaded, 16)
            sp.wait_ge(y_ready, TILES)
            sp.dma_start(out.rearrange("b o -> o b"), yrow[0:1, :]).then_inc(y_stored, 16)
            sp.wait_ge(y_stored, 16)

        @block.gpsimd
        def _(pool):
            nc.gpsimd.memset(corrO[:, :, :, :], 0.0).then_inc(corrO_zero, 1)
            pool.wait_ge(ids_loaded, 16)
            for t in range(TILES):
                if t >= EMB_RING:
                    pool.wait_ge(et_ready, t - EMB_RING + 1)
                for f in range(F):
                    pool.indirect_dma_start(
                        out=emb[:, t % EMB_RING, f * D:(f + 1) * D], out_offset=None, in_=tables[f][:, :],
                        in_offset=bass.IndirectOffsetOnAxis(ap=idx[:, t, f:f + 1], axis=0),
                    ).then_inc(gathered[t % EMB_RING], 16)

        @block.scalar
        def _(act):
            def setup_copy(n, dst, rows=P):
                act.wait_ge(setup_mm, n + 1)
                nc.scalar.copy(dst, setup_ps[n % 6][0:rows, :]).then_inc(setup_act, 1)

            def spread(u, ring):
                for q in range(Q):
                    lo, hi = q * D, (q + 1) * D
                    nc.scalar.copy(view(E, ring * UB * Q * F + q * F, [[Q * F, UB], [QTR, 4], [1, QTR]], (lo, hi)),
                                   view(ET, u * UB, [[1, UB], [EXT * BB, 4], [BB, QTR]], (lo, hi)))
                nc.scalar.copy(view(z2, ring * UB * 2 * F + F, [[2 * F, UB], [QTR, 4], [1, QTR]]),
                               view(ET, u * UB, [[1, UB], [EXT * BB, 4], [BB, QTR]])).then_inc(e_ready, 1)

            def empty(u, c, group):
                col = (u * UB + c * GB) * Q
                act.wait_ge(t_formed, group)
                for part in range(2):
                    nc.scalar.copy(*sg_copy(0, part, c, col))
                nc.scalar.copy(*own_copy(0, c, col))
                nc.scalar.copy(*x_copy(0, c, col)).then_inc(t_act, 1)

            def mlp_input(t):
                act.wait_ge(acc_ready, t + 1)
                nc.scalar.copy(xd[:, :], denseT[:, bass.ts(t, P)])
                nc.scalar.copy(x[:, :, :], acc_ps[:, 0:2 * P].rearrange("p (k b) -> p k b", k=2)).then_inc(x_ready, 1)

            def mlp_hidden1(t):
                act.wait_ge(h1_mm, t + 1)
                for m in range(M1):
                    last = nc.scalar.activation(h1[:, m, :], hid_ps[:, m * P:(m + 1) * P], ACT.Relu, bias=bt1[:, m:m + 1])
                last.then_inc(h1_ready, 1)

            def mlp_hidden2(t):
                act.wait_ge(h2_mm, t + 1)
                for m in range(M2):
                    last = nc.scalar.activation(h2[:, m, :], hid_ps[:, m * P:(m + 1) * P], ACT.Relu, bias=bt2[:, m:m + 1])
                last.then_inc(h2_ready, 1)

            def mlp_output(t):
                act.wait_ge(y_mm, t + 1)
                nc.scalar.copy(yrow[0:1, bass.ts(t, P)].rearrange("o (q b) -> o b q", q=Q),
                               hid_ps[0:1, 0:P].rearrange("o (b q) -> o b q", q=Q)).then_inc(y_ready, 1)

            def tile(t, first):
                act.wait_ge(et_ready, t + 1)
                for u in range(UNITS):
                    if not (first and u < 2):
                        act.wait_ge(t_formed, 2 * (t * UNITS + u) - 2)
                    spread(u, u % 2)
                    if first and u == 1:
                        for s in range(2):
                            act.wait_ge(half_stored[s], 16 * STORES_HALF)
                    if not first:
                        if u == 1:
                            mlp_input(t - 1)
                        if u == 3:
                            mlp_hidden1(t - 1)
                    if u >= 1:
                        for c in range(2):
                            empty(u - 1, c, 2 * (t * UNITS + u - 1) + c + 1)
                for c in range(2):
                    empty(UNITS - 1, c, 2 * (t * UNITS + UNITS - 1) + c + 1)
                if not first:
                    mlp_hidden2(t - 1)
                    mlp_output(t - 1)

            setup_copy(0, w0T[:, 0:BANK])
            setup_copy(N_DENSE, denseT[:, :], NX)
            for s in range(2):
                for w in range(QUARTER_BANKS):
                    setup_copy(quarter_bank(s, w), cross_q[:, s * QTR * C + w * BANK:s * QTR * C + (w + 1) * BANK])
                for r in range(2):
                    for w in range(HALF // WPB):
                        setup_copy(cross_bank(s, r, w), view(cross, (s * 2 + r) * HALF * C + w * BANK, [[1, BANK]]))
            for n in range(N_OWN, N_X):
                setup_copy(n, view(VO, (n - N_OWN) * BANK, [[1, BANK]]))
            for n in range(N_X, N_SQ):
                setup_copy(n, view(VX, (n - N_X) * BANK, [[1, BANK]], (0, PAIRS)), PAIRS)
            for n in range(N_SQ, N_SETUP):
                setup_copy(n, view(VS, (n - N_SQ) * BANK, [[1, BANK]]))
            act.wait_ge(E_zero, 1)
            tile(0, True)
            act.wait_ge(mlp_loaded, 16 * MLP_LOADS)
            with act.Fori(1, TILES) as t:
                tile(t, False)
            mlp_input(TILES - 1)
            mlp_hidden1(TILES - 1)
            mlp_hidden2(TILES - 1)
            mlp_output(TILES - 1)

        @block.vector
        def _(dve):
            def correct_x(s):
                dve.wait_ge(corrX_loaded[s], 16 * LOADS_HALF)
                for which in range(2):
                    v = VX[0:PAIRS, s, :, :]
                    nc.vector.tensor_tensor(v, v, corrX[0:PAIRS, s, which, :, :], ALU.add).then_inc(v_x, 1)
                    dve.wait_ge(v_x, 2 * s + which + 1)

            def correct_own():
                dve.wait_ge(corrO_loaded, 16 * 4 * LOADS_QUARTER)
                for which in range(2):
                    nc.vector.tensor_tensor(VO[:, :, :], VO[:, :, :], corrO[:, which, :, :], ALU.add).then_inc(v_own, 1)
                    dve.wait_ge(v_own, which + 1)

            def transpose_tile(t, slot, gathers):
                dve.wait_ge(gathered[slot], gathers)
                for g in range(4):
                    nc.vector.transpose(view(ET, g * EXT * BB, [[1, QTR * BB]]), emb[:, slot, g * QTR * D:(g + 1) * QTR * D])
                    last = nc.vector.transpose(view(ET, (g * EXT + QTR) * BB, [[1, ROT * BB]]),
                                               emb[:, slot, g * QTR * D:(g * QTR + ROT) * D])
                last.then_inc(et_ready, 1)
                dve.wait_ge(et_ready, t + 1)

            def products(u, ring):
                o, zo = u * UB, ring * UB * 2 * PAIRS
                for g in range(4):
                    pairs = g // 2 * PAIRS + g % 2 * QPAIRS
                    nc.vector.tensor_tensor(
                        view(z, zo + pairs, [[2 * PAIRS, UB], [QTR, ROT - 1], [1, QTR]]),
                        view(ET, g * EXT * BB + o, [[1, UB], [0, ROT - 1], [BB, QTR]]),
                        view(ET, g * EXT * BB + BB + o, [[1, UB], [BB, ROT - 1], [BB, QTR]]), ALU.mult)
                for s in range(2):
                    nc.vector.tensor_tensor(
                        view(z, zo + s * PAIRS + QTR * (ROT - 1), [[2 * PAIRS, UB], [QPAIRS, 2], [1, ROT]]),
                        view(ET, 2 * s * EXT * BB + o, [[1, UB], [EXT * BB, 2], [BB, ROT]]),
                        view(ET, (2 * s * EXT + ROT) * BB + o, [[1, UB], [EXT * BB, 2], [BB, ROT]]), ALU.mult)
                    nc.vector.tensor_tensor(
                        view(z, zo + s * PAIRS + 2 * QPAIRS, [[2 * PAIRS, UB], [QTR, QTR], [1, QTR]]),
                        view(ET, 2 * s * EXT * BB + o, [[1, UB], [BB, QTR], [0, QTR]]),
                        view(ET, (2 * s + 1) * EXT * BB + o, [[1, UB], [0, QTR], [BB, QTR]]), ALU.mult)
                e = view(ET, o, [[1, UB], [EXT * BB, 4], [BB, QTR]])
                nc.vector.tensor_tensor(view(z2, ring * UB * 2 * F, [[2 * F, UB], [QTR, 4], [1, QTR]]),
                                        e, e, ALU.mult).then_inc(z_ready, 1)

            def empty(u, c, group):
                col = (u * UB + c * GB) * Q
                dve.wait_ge(t_formed, group)
                for part in range(2):
                    nc.vector.tensor_copy(*sg_copy(1, part, c, col))
                nc.vector.tensor_copy(*own_copy(1, c, col))
                nc.vector.tensor_copy(*x_copy(1, c, col)).then_inc(t_dve, 1)

            def tile(t, slot, gathers, first):
                if not first:
                    dve.wait_ge(e_ready, t * UNITS)
                transpose_tile(t, slot, gathers)
                for u in range(UNITS):
                    if not (first and u < 2):
                        dve.wait_ge(t_formed, 2 * (t * UNITS + u) - 2)
                    products(u, u % 2)
                    if first and u == 1:
                        for s in range(2):
                            dve.wait_ge(half_stored[s], 16 * STORES_HALF)
                    if u >= 1:
                        for c in range(2):
                            empty(u - 1, c, 2 * (t * UNITS + u - 1) + c + 1)
                    if first and u == 2:
                        dve.wait_ge(setup_act, act_banks(N_SETUP - 1))
                        correct_x(0)
                if first:
                    correct_own()
                for c in range(2):
                    empty(UNITS - 1, c, 2 * (t * UNITS + UNITS - 1) + c + 1)
                if first:
                    correct_x(1)
                    nc.vector.tensor_tensor(VS[:, :, :], VS[:, :, :], corrS[:, :, :], ALU.add).then_inc(v_squares, 1)

            nc.vector.memset(corrS[:, :, :], 0.0).then_inc(corrS_zero, 1)
            nc.vector.memset(E[:, :, :, :], 0.0).then_inc(E_zero, 1)
            nc.vector.memset(w0own[:, :, :], 0.0).then_inc(w0own_zero, 1)
            dve.wait_ge(setup_mm, 2)
            nc.vector.tensor_copy(w0T[:, BANK:2 * BANK], setup_ps[1][:, :]).then_inc(setup_dve, 1)
            dve.wait_ge(setup_act, 1)
            dve.wait_ge(setup_dve, 1)
            for s in range(2):
                nc.vector.tensor_tensor(w0x[:, s, :, :],
                                        view(w0T, s * HALF * F + (1 - s) * HALF, [[F, HALF], [1, HALF]]),
                                        view(w0T, (1 - s) * HALF * F + s * HALF, [[1, HALF], [F, HALF]]), ALU.add)
            for u in range(2):
                last = nc.vector.tensor_tensor(
                    view(w0xq, u * QTR * QTR, [[2 * QTR * QTR, 2], [QTR, QTR], [1, QTR]]),
                    view(w0T, u * QTR * F + (1 - u) * QTR, [[HALF * (F + 1), 2], [F, QTR], [1, QTR]]),
                    view(w0T, (1 - u) * QTR * F + u * QTR, [[HALF * (F + 1), 2], [1, QTR], [F, QTR]]), ALU.add)
            last.then_inc(w0x_ready, 1)
            for q0, q1 in ((0, QTR), (QTR, EXT)):
                last = nc.vector.tensor_tensor(
                    view(w0sym, q0, [[QTR * EXT, 4], [EXT, QTR], [1, q1 - q0]]),
                    view(w0T, 0, [[QTR * (F + 1), 4], [F, QTR], [1, q1 - q0]]),
                    view(w0T, 0, [[QTR * (F + 1), 4], [1, QTR], [F, q1 - q0]]), ALU.add)
            last.then_inc(w0sym_ready, 1)
            dve.wait_ge(w0sym_ready, 1)
            dve.wait_ge(w0x_ready, 1)
            for s in range(2):
                nc.vector.tensor_copy(view(w0pair, s * PAIRS, [[QPAIRS, 2], [QTR, ROT - 1], [1, QTR]]),
                                      view(w0sym, 2 * s * QTR * EXT + 1, [[QTR * EXT, 2], [1, ROT - 1], [EXT + 1, QTR]]))
            nc.vector.tensor_copy(view(w0pair, QTR * (ROT - 1), [[PAIRS, 2], [QPAIRS, 2], [1, ROT]]),
                                  view(w0sym, ROT, [[2 * QTR * EXT, 2], [QTR * EXT, 2], [EXT + 1, ROT]]))
            nc.vector.tensor_copy(w0pair[:, :, 2 * QPAIRS:PAIRS], view(w0xq, 0, [[2 * QTR * QTR, 2], [1, QTR * QTR]]))\
              .then_inc(w0pair_ready, 1)
            dve.wait_ge(w0pair_ready, 1)
            dve.wait_ge(w0own_zero, 1)
            nc.vector.tensor_copy(w0own[:, :, 0:2 * QPAIRS], w0pair[:, :, 0:2 * QPAIRS]).then_inc(w0own_ready, 1)
            tile(0, 0, 16 * F, True)
            tile(1, 1, 16 * F, False)
            with dve.Fori(1, TILES // EMB_RING) as i:
                for slot in range(EMB_RING):
                    tile(i * EMB_RING + slot, slot, (i + 1) * (16 * F), False)

        @block.tensor
        def _(pe):
            def setup_bank(n):
                if n - 6 == 1:
                    pe.wait_ge(setup_dve, 1)
                elif n >= 6:
                    pe.wait_ge(setup_act, act_banks(n - 6))
                return setup_ps[n % 6]

            def w1_fields(h):
                return w1[:, h:h + WPB, :].rearrange("m w j -> m (w j)")

            def form(u, t, first):
                ring = u % 2
                pe.wait_ge(z_ready, t * UNITS + u + 1)
                pe.wait_ge(e_ready, t * UNITS + u + 1)
                for c in range(2):
                    if not (first and u == 0):
                        pe.wait_ge(t_act, 2 * (t * UNITS + u) + c - 1)
                        pe.wait_ge(t_dve, 2 * (t * UNITS + u) + c - 1)
                    for b in range(GB):
                        bb = c * GB + b
                        for s in range(2):
                            nc.tensor.matmul(pair_ps[s][c][0:PAIRS, b * Q * F:(b + 1) * Q * F],
                                             z[:, ring, bb, s * PAIRS:(s + 1) * PAIRS], E[:, ring, bb, :],
                                             start=True, stop=True)
                    for b in range(GB):
                        bb = c * GB + b
                        for g in range(2):
                            for half in range(2):
                                row = 32 * (2 * g + half)
                                last = nc.tensor.matmul(
                                    sg_ps[c][row:row + F, b * Q * HALF:(b + 1) * Q * HALF], z2[:, ring, bb, g * F:(g + 1) * F],
                                    view(E, (ring * UB + bb) * Q * F + half * HALF, [[F, Q], [1, HALF]]),
                                    start=True, stop=True)
                    last.then_inc(t_formed, 1)

            def contract(t, wait_v, between):
                def t_part(offset):
                    return view(T, offset, [[1, P]])
                out1, out2 = acc_ps[:, 0:P], acc_ps[:, P:2 * P]
                pe.wait_ge(t_act, 2 * UNITS * (t + 1))
                pe.wait_ge(t_dve, 2 * UNITS * (t + 1))
                if wait_v:
                    pe.wait_ge(v_own, 2)
                for h in range(HALF):
                    nc.tensor.matmul(out2, VO[:, h, :], t_part(TOWN + h * P), start=(h == 0), stop=False)
                if between:
                    between()
                for s in range(2):
                    if wait_v:
                        pe.wait_ge(v_x, 2 * (s + 1))
                    for h in range(HALF):
                        nc.tensor.matmul(out2, VX[0:PAIRS, s, h, :], view(T, TX + (s * HALF + h) * P, [[1, P]], (0, PAIRS)),
                                         start=False, stop=False)
                if wait_v:
                    pe.wait_ge(v_squares, 1)
                for h in range(QTR):
                    nc.tensor.matmul(out2, VS[:, h, :], t_part(TSG + h * P), start=False, stop=(h == QTR - 1))
                if wait_v:
                    pe.wait_ge(w0g_loaded, 16 * 4)
                for h in range(QTR):
                    last = nc.tensor.matmul(out1, W0g[:, h, :], t_part(TSG + (QTR + h) * P), start=(h == 0), stop=(h == QTR - 1))
                last.then_inc(acc_ready, 1)

            def mlp1(t):
                pe.wait_ge(x_ready, t + 1)
                for m in range(M1):
                    o = hid_ps[:, m * P:(m + 1) * P]
                    for k in range(2):
                        nc.tensor.matmul(o, wt1[:, k, m * P:(m + 1) * P], x[:, k, :], start=(k == 0), stop=False)
                    last = nc.tensor.matmul(o, wt1d[:, m * P:(m + 1) * P], xd[:, :], start=False, stop=True)
                last.then_inc(h1_mm, 1)

            def mlp2(t):
                pe.wait_ge(h1_ready, t + 1)
                for m in range(M2):
                    for k in range(M1):
                        last = nc.tensor.matmul(hid_ps[:, m * P:(m + 1) * P], wt2[:, k, m * P:(m + 1) * P],
                                                h1[:, k, :], start=(k == 0), stop=(k == M1 - 1))
                last.then_inc(h2_mm, 1)

            def mlp3(t):
                pe.wait_ge(h2_ready, t + 1)
                for k in range(M2):
                    last = nc.tensor.matmul(hid_ps[0:1, 0:P], wt3[:, k:k + 1], h2[:, k, :], start=(k == 0), stop=(k == M2 - 1))
                last.then_inc(y_mm, 1)

            pe.wait_ge(ident_loaded, 16)
            pe.wait_ge(w0_loaded, 16)
            for n in range(N_W0T):
                for i in range(BANK // P):
                    last = nc.tensor.transpose(setup_ps[n][:, i * P:(i + 1) * P], w0[:, n * (BANK // P) + i, :], ident[:, :])
                last.then_inc(setup_mm, 1)
            pe.wait_ge(dense_loaded, 16 * TILES)
            for t in range(TILES):
                last = nc.tensor.transpose(setup_ps[N_DENSE][0:NX, t * P:(t + 1) * P], dense_in[:, t, :], ident[:, :])
            last.then_inc(setup_mm, 1)
            pe.wait_ge(w0x_ready, 1)
            for s in range(2):
                for n in range(s * (HALF // WPB), (s + 1) * (HALF // WPB)):
                    pe.wait_ge(w1_loaded[n], 16)
                for w in range(QUARTER_BANKS):
                    ps = setup_bank(quarter_bank(s, w))
                    for u in range(2):
                        last = nc.tensor.matmul(ps[64 * u:64 * u + 64, :], w0xq[:, s, u, :, :].rearrange("m o t -> m (o t)"),
                                                w1_fields((2 * s + u) * QTR + w * WPB), start=True, stop=True)
                    last.then_inc(setup_mm, 1)
                for r in range(2):
                    for w in range(HALF // WPB):
                        nc.tensor.matmul(setup_bank(cross_bank(s, r, w))[:, :],
                                         w0x[:, s, r * QTR:(r + 1) * QTR, :].rearrange("m o t -> m (o t)"),
                                         w1_fields(s * HALF + w * WPB), start=True, stop=True).then_inc(setup_mm, 1)
            pe.wait_ge(w0own_ready, 1)
            for w in range(HALF // WPB):
                ps = setup_bank(N_OWN + w)
                for s in range(2):
                    last = nc.tensor.matmul(ps[64 * s:64 * s + 64, :], w0own[:, s, :],
                                            w1_fields(s * HALF + w * WPB), start=True, stop=True)
                last.then_inc(setup_mm, 1)
            for s in range(2):
                for w in range(HALF // WPB):
                    nc.tensor.matmul(setup_bank(N_X + s * (HALF // WPB) + w)[0:PAIRS, :], w0pair[:, s, :],
                                     w1_fields((1 - s) * HALF + w * WPB), start=True, stop=True).then_inc(setup_mm, 1)
            for w in range(QTR // WPB):
                ps = setup_bank(N_SQ + w)
                for j, quarter in enumerate(QUARTER_OF_BLOCK):
                    last = nc.tensor.matmul(ps[32 * j:32 * j + F, :], w0T[:, 0:F * F:F + 1],
                                            w1_fields(quarter * QTR + w * WPB), start=True, stop=True)
                last.then_inc(setup_mm, 1)
            pe.wait_ge(setup_act, act_banks(N_SETUP - 1))

            for u in range(UNITS):
                form(u, 0, True)
            contract(0, True, None)
            pe.wait_ge(mlp_loaded, 16 * MLP_LOADS)
            with pe.Fori(1, TILES) as t:
                form(0, t, False)
                form(1, t, False)
                mlp1(t - 1)
                form(2, t, False)
                form(3, t, False)
                mlp2(t - 1)
                contract(t, False, lambda: mlp3(t - 1))
            mlp1(TILES - 1)
            mlp2(TILES - 1)
            mlp3(TILES - 1)


def kernel(**inputs):
    import numpy as np
    import concourse.bacc as bacc
    from concourse.bass_utils import run_bass_kernel_spmd

    nc = bacc.Bacc("TRN2", target_bir_lowering=False, num_devices=1)
    arrays = {}

    def given(name, array):
        array = np.ascontiguousarray(array)
        arrays[name] = array
        return nc.dram_tensor(name, array.shape, mybir.dt.from_np(array.dtype), kind="ExternalInput").ap()

    ids = given("ids_in", inputs["ids"])
    tables = [given(f"tbl_{f}_in", inputs[f"tbl_{f}"]) for f in range(F)]
    by_partition = {name: np.asarray(inputs[name]).reshape(-1, P).T for name in ("b_top1", "b_top2", "W_top3")}
    args = [given(name + "_in", by_partition.get(name, inputs[name])) for name in
            ("L0_rec_W0", "L0_rec_W1", "W_top1", "b_top1", "W_top2", "b_top2", "W_top3", "dense_ctx")]
    identity = given("identity_in", np.eye(P, dtype=np.float32))
    out = nc.dram_tensor("out_y", (ids.shape[0], 1), mybir.dt.float32, kind="ExternalOutput").ap()
    scratch = [nc.dram_tensor(f"cross_scratch{s}", (2 * EXT, 2 * EXT, HALF, C), mybir.dt.float32, kind="Internal").ap()
               for s in range(2)]
    scratch_q = [nc.dram_tensor(f"cross_scratch_quarter{g}", (EXT, EXT, QTR, C), mybir.dt.float32, kind="Internal").ap()
                 for g in range(4)]
    build(nc, ids, tables, *args, identity, out, scratch, scratch_q)
    result = run_bass_kernel_spmd(nc, [arrays], core_ids=[0])
    return result.results[0]["out_y"]
```

```python
import concourse.bass as bass
from concourse import mybir
from contextlib import ExitStack

P = 128
F = 32
D = 32
C = 128
HALF = F // 2
QTR = F // 4
ROT = QTR // 2
EXT = QTR + ROT
QPAIRS = QTR * ROT
OWN = 2 * QPAIRS
PAIRS = OWN + QTR * QTR
Q = P // D
BB = P // Q
UB = 8
UNITS = BB // UB
GB = 4
QUARTER_OF_BLOCK = [0, 2, 1, 3]
BANK = 512
EMB_RING = 2


def build(nc, ids, tables, W0, W1, W_top1, b_top1, W_top2, b_top2, W_top3, dense, identity, out, scratch, scratch_q):
    fp32, i32 = mybir.dt.float32, mybir.dt.int32
    ALU, ACT = mybir.AluOpType, mybir.ActivationFunctionType
    B = ids.shape[0]
    TILES = B // P
    NX = dense.shape[1]
    H1, H2 = W_top1.shape[1], W_top2.shape[1]
    M1, M2 = H1 // P, H2 // P

    ctx = ExitStack()
    with ctx:
        def sb(name, shape, dt=fp32):
            return ctx.enter_context(nc.sbuf_tensor(name, shape, dt))

        def sem(name):
            return ctx.enter_context(nc.semaphore(name))

        def view(handle, offset, dims, part=None):
            whole = handle[tuple(slice(None) for _ in handle.shape)] if part is None else \
                handle[(slice(*part),) + tuple(slice(None) for _ in handle.shape[1:])]
            return bass.AP(whole.tensor, whole.offset + offset, [list(whole.ap[0])] + dims)

        idx = sb("idx", [P, TILES, F], i32)
        emb = sb("emb", [P, EMB_RING, F * D])
        ET = sb("ET", [P, 4, EXT, BB])
        z = sb("z", [P, 2, UB, 2 * PAIRS])
        z2 = sb("z2", [P, 2, UB, 2 * F])
        E = sb("E", [P, 2, UB, Q * F])
        T = sb("T", [P, 4 * HALF * P])
        TX, TOWN, TSG = 0, 2 * HALF * P, 3 * HALF * P
        VX = sb("VX", [P, 2, HALF, C])
        VO = sb("VO", [P, HALF, C])
        VS = sb("VS", [P, QTR, C])
        W0g = sb("W0g", [P, QTR, C])
        w1 = sb("w1", [P, F, C])
        w0T = sb("w0T", [P, F * F])
        w0x = sb("w0x", [P, 2, HALF, HALF])
        w0xq = sb("w0xq", [P, 2, 2, QTR, QTR])
        w0sym = sb("w0sym", [P, 4, QTR, EXT])
        w0pair = sb("w0pair", [P, 2, PAIRS])
        corrX = sb("corrX", [P, 2, 2, HALF, C])
        corrO = sb("corrO", [P, 2, HALF, C])
        corrS = sb("corrS", [P, QTR, C])
        ident = sb("ident", [P, P])
        dense_in = sb("dense_in", [P, TILES, NX])
        denseT = sb("denseT", [NX, B])
        wt3 = sb("wt3", [P, M2])
        bt1 = sb("bt1", [P, M1])
        bt2 = sb("bt2", [P, M2])
        x = sb("x", [P, 2, P])
        xd = sb("xd", [NX, P])
        yrow = sb("yrow", [1, B])
        w0 = view(corrX, 0, [[C, F * F // P], [1, C]])
        mlp_room = [0, 2 * M1, 3 * M1, 3 * M1 + M1 * M2, 4 * M1 + M1 * M2, 4 * M1 + M1 * M2 + M2]
        wt1, wt1d, wt2, h1, h2 = (w1[:, lo:hi, :] for lo, hi in zip(mlp_room, mlp_room[1:]))
        wt1 = wt1.rearrange("p (k m) c -> p k (m c)", k=2)
        wt1d = wt1d[0:NX, :, :].rearrange("p m c -> p (m c)")
        wt2 = wt2.rearrange("p (k m) c -> p k (m c)", k=M1)
        cross = T
        cross_q = view(corrX, 2 * HALF * C, [[1, 2 * QTR * C]])

        def bank(name):
            return ctx.enter_context(nc.psum_tensor(name, [P, BANK], fp32))
        pair_ps = [[bank(f"pair{s}_{c}") for c in range(2)] for s in range(2)]
        sg_ps = [bank(f"sg_{c}") for c in range(2)]
        acc_ps = bank("acc")
        hid_ps = bank("hid")
        setup_ps = [pair_ps[0][0], pair_ps[0][1], pair_ps[1][1], sg_ps[1], pair_ps[1][0], sg_ps[0]]

        squares_ps = [acc_ps, hid_ps]
        last_h1_ps = [pair_ps[0][0], pair_ps[0][1], pair_ps[1][0], pair_ps[1][1]]
        last_h2_ps = sg_ps
        assert (M1, M2) == (len(last_h1_ps), len(last_h2_ps))

        def x_copy(s, c, col):
            return (view(T, TX + s * HALF * P + col, [[1, GB * Q], [P, HALF]], (0, PAIRS)),
                    view(pair_ps[s][c], (1 - s) * HALF, [[F, GB * Q], [1, HALF]], (0, PAIRS)))

        def own_copy(s, c, col):
            return (view(T, TOWN + col, [[1, GB * Q], [P, HALF]], (s * OWN, (s + 1) * OWN)),
                    view(pair_ps[s][c], s * HALF, [[F, GB * Q], [1, HALF]], (0, OWN)))

        def sg_copy(g, part, c, col):
            return (view(T, TSG + g * QTR * P + col, [[1, GB * Q], [P, QTR]], (64 * part, 64 * part + 64)),
                    view(sg_ps[c], part * QTR, [[HALF, GB * Q], [1, QTR]], (64 * g, 64 * g + 64)))

        ids_loaded = sem("ids_loaded")
        w0_loaded = [sem(f"w0_loaded{n}") for n in range(2)]
        ident_loaded = sem("ident_loaded")
        w1_loaded = [sem(f"w1_loaded{n}") for n in range(F * C // BANK)]
        dense_loaded = sem("dense_loaded")
        w0g_loaded = sem("w0g_loaded")
        mlp_loaded = sem("mlp_loaded")
        gathered = [[sem(f"gathered{i}_{g}") for g in range(4)] for i in range(EMB_RING)]
        setup_mm = sem("setup_mm")
        squares_mm = sem("squares_mm")
        squares_act = sem("squares_act")
        dense_act = sem("dense_act")
        dense_mm = sem("dense_mm")
        setup_act = sem("setup_act")
        setup_dve = sem("setup_dve")
        w0x_ready = sem("w0x_ready")
        w0sym_ready = sem("w0sym_ready")
        w0pair_ready = sem("w0pair_ready")
        corr_zero = sem("corr_zero")
        w0pair_zero = sem("w0pair_zero")
        E_zero = sem("E_zero")
        quarters_stored = [sem(f"quarters_stored{s}") for s in range(2)]
        half_stored = [[sem(f"half_stored{s}_{r}") for r in range(2)] for s in range(2)]
        corrX_loaded = [sem(f"corrX_loaded{s}") for s in range(2)]
        corrO_loaded = sem("corrO_loaded")
        v_x = sem("v_x")
        v_own = sem("v_own")
        v_squares = sem("v_squares")
        et_ready = sem("et_ready")
        z_ready = [sem(f"z_ready{s}") for s in range(2)]
        e_ready = sem("e_ready")
        t_formed = sem("t_formed")
        t_act = sem("t_act")
        sg_emptied = sem("sg_emptied")
        t_dve = sem("t_dve")
        acc_ready = sem("acc_ready")
        x_ready = sem("x_ready")
        h1_mm = sem("h1_mm")
        h1_ready = sem("h1_ready")
        h2_mm = sem("h2_mm")
        h2_ready = sem("h2_ready")
        last_h1_mm = sem("last_h1_mm")
        last_h1_act = sem("last_h1_act")
        last_h1_dve = sem("last_h1_dve")
        last_h2_mm = sem("last_h2_mm")
        last_h2_act = sem("last_h2_act")
        last_h2_dve = sem("last_h2_dve")
        y_mm = sem("y_mm")
        y_ready = sem("y_ready")
        y_stored = sem("y_stored")

        WPB = BANK // C
        N_W0T = F * F // BANK
        N_CROSS = N_W0T
        QUARTER_BANKS = QTR // WPB
        CROSS_BANKS = QUARTER_BANKS + 2 * HALF // WPB
        N_X = N_CROSS + 2 * CROSS_BANKS
        N_OWN = N_X + 2 * HALF // WPB
        N_SETUP = N_OWN + HALF // WPB
        assert N_SETUP % 6 == 4

        def act_banks(n):
            return n if n > 1 else n + 1

        def cross_bank(s, r, w):
            return N_CROSS + s * CROSS_BANKS + r * (HALF // WPB) + w

        def quarter_bank(s, w):
            return cross_bank(s, 2, w)

        MLP_LOADS = 6
        STORES_QUARTER, STORES_PART = 3, 4
        LOADS_QUARTER, LOADS_HALF = 3, 8

        block = ctx.enter_context(nc.Block())

        @block.sync
        def _(sp):
            sp.dma_start(idx[:, :, :], ids.rearrange("(t p) f -> p t f", p=P)).then_inc(ids_loaded, 16)
            sp.dma_start(ident[:, :], identity).then_inc(ident_loaded, 16)
            for n in range(2):
                rows = slice(n * BANK // P, (n + 1) * BANK // P)
                sp.dma_start(w0[:, rows, :], W0.rearrange("(t p) c -> p t c", p=P)[:, rows, :]).then_inc(w0_loaded[n], 16)
            for n in range(F // WPB):
                sp.dma_start(w1[:, n * WPB:(n + 1) * WPB, :],
                             W1.rearrange("(h m) j -> m h j", m=C)[:, n * WPB:(n + 1) * WPB, :]).then_inc(w1_loaded[n], 16)
            for t in range(TILES):
                sp.dma_start(dense_in[:, t, :],
                             dense[t * P:(t + 1) * P, :].rearrange("(q b) n -> b q n", q=Q)).then_inc(dense_loaded, 16)
            for j, quarter in enumerate(QUARTER_OF_BLOCK):
                sp.dma_start(W0g[32 * j:32 * j + F, :, :],
                             W0.rearrange("(f h) c -> f h c", h=F)[:, quarter * QTR:(quarter + 1) * QTR, :])\
                  .then_inc(w0g_loaded, 16)

            def store(dst, src, stored):
                sp.dma_start(dst.rearrange("w o t j -> (o t) w j"), src).then_inc(stored, 16)

            def store_quarters(s):
                sp.wait_ge(setup_act, act_banks(quarter_bank(s, QUARTER_BANKS - 1)))
                for u in range(2):
                    cells, done = scratch_q[2 * s + u], quarters_stored[s]
                    src = cross_q[u * 64:(u + 1) * 64, s * QTR * C:(s + 1) * QTR * C].rearrange("p (w j) -> p w j", j=C)
                    store(cells[0:QTR, 0:QTR, :, :], src, done)
                    store(cells[QTR:EXT, 0:QTR, :, :], src[:, 0:ROT, :], done)
                    store(cells[0:QTR, QTR:EXT, :, :], src[0:ROT * QTR, :, :], done)

            def store_half(s, r):
                sp.wait_ge(setup_act, act_banks(cross_bank(s, r, HALF // WPB - 1)))
                cells, done = scratch[s], half_stored[s][r]
                src = cross[:, (s * 2 + r) * HALF * C:(s * 2 + r + 1) * HALF * C].rearrange("p (w j) -> p w j", j=C)
                o = r * EXT
                for u in range(2):
                    store(cells[u * EXT:u * EXT + QTR, o:o + QTR, :, :], src[:, u * QTR:(u + 1) * QTR, :], done)
                own = src[:, r * QTR:(r + 1) * QTR, :]
                store(cells[o + QTR:o + EXT, o:o + QTR, :, :], own[:, 0:ROT, :], done)
                store(cells[o:o + QTR, o + QTR:o + EXT, :, :], own[0:ROT * HALF, :, :], done)

            def load_rotations(dst, row, cells, off, so, sw, width, loaded):
                for which, step, rotations in ((0, so, ROT), (1, sw, ROT - 1)):
                    sp.dma_start(dst[row:row + rotations * QTR, which, :, :].rearrange("r t j -> r (t j)"),
                                 bass.AP(cells.tensor, off + step, [[step, rotations], [so + sw, QTR], [1, width]]))\
                      .then_inc(loaded, 16)

            def load_quarter(g):
                so, sw = QTR * C, EXT * QTR * C
                cells = scratch_q[g][:, :, :, :]
                other = (1 - g % 2) * QTR
                load_rotations(corrO[:, :, other:other + QTR, :], g * QPAIRS, cells, 0, so, sw, QTR * C, corrO_loaded)
                row = 32 * QUARTER_OF_BLOCK[g + 1 - 2 * (g % 2)] + g * QTR
                sp.dma_start(corrS[row:row + QTR, :, :].rearrange("r t j -> r (t j)"),
                             bass.AP(cells.tensor, 0, [[so + sw, QTR], [1, QTR * C]])).then_inc(corrO_loaded, 16)

            def load_half(s):
                so, sw = HALF * C, 2 * EXT * HALF * C
                cells = scratch[s][:, :, :, :]
                for u in range(2):
                    load_rotations(corrX[:, s, :, :, :], u * QPAIRS, cells, u * EXT * (so + sw), so, sw, HALF * C,
                                   corrX_loaded[s])
                for which, step_p, step_q in ((0, sw, so), (1, so, sw)):
                    sp.dma_start(corrX[OWN:PAIRS, s, which, :, :].rearrange("r t j -> r (t j)"),
                                 bass.AP(cells.tensor, EXT * step_q, [[step_p, QTR], [step_q, QTR], [1, HALF * C]]))\
                      .then_inc(corrX_loaded[s], 16)
                for v in range(2):
                    row = 32 * QUARTER_OF_BLOCK[2 * (1 - s) + v] + s * HALF
                    sp.dma_start(corrS[row:row + HALF, :, :].rearrange("r t j -> r (t j)"),
                                 bass.AP(cells.tensor, v * QTR * C, [[EXT * (so + sw), 2], [so + sw, QTR], [1, QTR * C]]))\
                      .then_inc(corrX_loaded[s], 16)

            for s in range(2):
                for r in range(2):
                    store_half(s, r)
            store_quarters(0)
            for g in range(4):
                sp.wait_ge(gathered[0][g], 16 * QTR)
            store_quarters(1)
            sp.wait_ge(corr_zero, 3)
            for r in range(2):
                sp.wait_ge(half_stored[0][r], 16 * STORES_PART)
            load_half(0)
            for s in range(2):
                sp.wait_ge(quarters_stored[s], 16 * 2 * STORES_QUARTER)
            for r in range(2):
                sp.wait_ge(half_stored[1][r], 16 * STORES_PART)
            load_half(1)
            load_quarter(0)
            load_quarter(1)
            load_quarter(2)
            load_quarter(3)
            sp.wait_ge(setup_mm, N_SETUP)
            sp.wait_ge(squares_mm, QTR // WPB)
            sp.dma_start(wt1[:, :, :], W_top1[0:2 * C, :].rearrange("(k p) n -> p k n", p=P)).then_inc(mlp_loaded, 16)
            sp.dma_start(wt1d[:, :], W_top1[2 * C:2 * C + NX, :]).then_inc(mlp_loaded, 16)
            sp.dma_start(wt2[:, :, :], W_top2.rearrange("(k p) n -> p k n", p=P)).then_inc(mlp_loaded, 16)
            sp.dma_start(wt3[:, :], W_top3).then_inc(mlp_loaded, 16)
            sp.dma_start(bt1[:, :], b_top1).then_inc(mlp_loaded, 16)
            sp.dma_start(bt2[:, :], b_top2).then_inc(mlp_loaded, 16)
            sp.wait_ge(y_ready, TILES)
            sp.dma_start(out.rearrange("b o -> o b"), yrow[0:1, :]).then_inc(y_stored, 16)
            sp.wait_ge(y_stored, 16)

        @block.gpsimd
        def _(pool):
            pool.wait_ge(ids_loaded, 16)
            for t in range(TILES):
                if t >= EMB_RING:
                    pool.wait_ge(et_ready, 2 * (t - EMB_RING + 1))
                for f in range(F):
                    pool.indirect_dma_start(
                        out=emb[:, t % EMB_RING, f * D:(f + 1) * D], out_offset=None, in_=tables[f][:, :],
                        in_offset=bass.IndirectOffsetOnAxis(ap=idx[:, t, f:f + 1], axis=0),
                    ).then_inc(gathered[t % EMB_RING][f // QTR], 16)
                if t == 1:
                    pool.wait_ge(squares_act, QTR // WPB)
                    pool.wait_ge(corrX_loaded[0], 16 * LOADS_HALF)
                    pool.wait_ge(corrO_loaded, 16 * 4 * LOADS_QUARTER)
                    nc.gpsimd.tensor_tensor(VS[:, :, :], VS[:, :, :], corrS[:, :, :], ALU.add).then_inc(v_squares, 1)

        @block.scalar
        def _(act):
            def setup_copy(n, dst, rows=P):
                act.wait_ge(setup_mm, n + 1)
                nc.scalar.copy(dst, setup_ps[n % 6][0:rows, :]).then_inc(setup_act, 1)

            def spread(u, ring):
                for q in range(Q):
                    lo, hi = q * D, (q + 1) * D
                    nc.scalar.copy(view(E, ring * UB * Q * F + q * F, [[Q * F, UB], [QTR, 4], [1, QTR]], (lo, hi)),
                                   view(ET, u * UB, [[1, UB], [EXT * BB, 4], [BB, QTR]], (lo, hi)))
                e = view(ET, u * UB, [[1, UB], [EXT * BB, 4], [BB, QTR]])
                nc.scalar.copy(view(z2, ring * UB * 2 * F + F, [[2 * F, UB], [QTR, 4], [1, QTR]]), e)
                nc.scalar.activation(view(z2, ring * UB * 2 * F, [[2 * F, UB], [QTR, 4], [1, QTR]]), e, ACT.Square)\
                  .then_inc(e_ready, 1)

            def spread_half(u, ring, s):
                for q in range(Q):
                    lo, hi = q * D, (q + 1) * D
                    nc.scalar.copy(view(E, ring * UB * Q * F + q * F + s * HALF, [[Q * F, UB], [QTR, 2], [1, QTR]], (lo, hi)),
                                   view(ET, 2 * s * EXT * BB + u * UB, [[1, UB], [EXT * BB, 2], [BB, QTR]], (lo, hi)))
                e = view(ET, 2 * s * EXT * BB + u * UB, [[1, UB], [EXT * BB, 2], [BB, QTR]])
                columns = ring * UB * 2 * F + s * HALF
                nc.scalar.copy(view(z2, columns + F, [[2 * F, UB], [QTR, 2], [1, QTR]]), e)
                last = nc.scalar.activation(view(z2, columns, [[2 * F, UB], [QTR, 2], [1, QTR]]), e, ACT.Square)
                if s == 1:
                    last.then_inc(e_ready, 1)

            def empty(u, c, group):
                col = (u * UB + c * GB) * Q
                act.wait_ge(t_formed, group)
                for g in range(2):
                    for part in range(2):
                        last = nc.scalar.copy(*sg_copy(g, part, c, col))
                last.then_inc(sg_emptied, 1)
                nc.scalar.copy(*own_copy(0, c, col))
                nc.scalar.copy(*x_copy(0, c, col)).then_inc(t_act, 1)

            def mlp_input(t, last=False):
                if not last:
                    nc.scalar.copy(xd[:, :], denseT[:, bass.ts(t, P)])
                act.wait_ge(acc_ready, t + 1)
                nc.scalar.copy(x[:, :, :], acc_ps[:, 0:2 * P].rearrange("p (k b) -> p k b", k=2)).then_inc(x_ready, 1)

            def mlp_hidden1(t):
                act.wait_ge(h1_mm, t + 1)
                for m in range(M1):
                    last = nc.scalar.activation(h1[:, m, :], hid_ps[:, m * P:(m + 1) * P], ACT.Relu, bias=bt1[:, m:m + 1])
                last.then_inc(h1_ready, 1)

            def mlp_hidden2(t):
                act.wait_ge(h2_mm, t + 1)
                for m in range(M2):
                    last = nc.scalar.activation(h2[:, m, :], hid_ps[:, m * P:(m + 1) * P], ACT.Relu, bias=bt2[:, m:m + 1])
                last.then_inc(h2_ready, 1)

            def mlp_output(t):
                act.wait_ge(y_mm, t + 1)
                nc.scalar.copy(yrow[0:1, bass.ts(t, P)].rearrange("o (q b) -> o b q", q=Q),
                               hid_ps[0:1, 0:P].rearrange("o (b q) -> o b q", q=Q)).then_inc(y_ready, 1)

            def tile(t, first):
                if not first:
                    act.wait_ge(et_ready, 2 * (t + 1))
                for u in range(UNITS):
                    if not (first and u < 2):
                        act.wait_ge(t_formed, 2 * (t * UNITS + u) - 2)
                    if not (first and u == 0):
                        spread(u, u % 2)
                    if first and u == 1:
                        for s in range(2):
                            for r in range(2):
                                act.wait_ge(half_stored[s][r], 16 * STORES_PART)
                    if not first:
                        if u == 1:
                            mlp_input(t - 1)
                        if u == 3:
                            mlp_hidden1(t - 1)
                    if u >= 1:
                        for c in range(2):
                            empty(u - 1, c, 2 * (t * UNITS + u - 1) + c + 1)
                for c in range(2):
                    empty(UNITS - 1, c, 2 * (t * UNITS + UNITS - 1) + c + 1)
                if not first:
                    mlp_hidden2(t - 1)
                    mlp_output(t - 1)

            setup_copy(0, w0T[:, 0:BANK])
            for s in range(2):
                for r in range(2):
                    for w in range(HALF // WPB):
                        setup_copy(cross_bank(s, r, w), view(cross, (s * 2 + r) * HALF * C + w * BANK, [[1, BANK]]))
                for w in range(QUARTER_BANKS):
                    setup_copy(quarter_bank(s, w), cross_q[:, s * QTR * C + w * BANK:s * QTR * C + (w + 1) * BANK])
            for n in range(N_X, N_OWN):
                setup_copy(n, view(VX, (n - N_X) * BANK, [[1, BANK]]))
            act.wait_ge(dense_mm, 1)
            nc.scalar.copy(denseT[:, :], hid_ps[0:NX, :]).then_inc(dense_act, 1)
            act.wait_ge(E_zero, 1)
            act.wait_ge(et_ready, 1)
            spread_half(0, 0, 0)
            for n in range(N_OWN, N_SETUP):
                setup_copy(n, view(VO, (n - N_OWN) * BANK, [[1, BANK]]))
            act.wait_ge(et_ready, 2)
            spread_half(0, 0, 1)
            for w, ps in enumerate(squares_ps):
                act.wait_ge(squares_mm, w + 1)
                nc.scalar.copy(view(VS, w * BANK, [[1, BANK]]), ps[:, :]).then_inc(squares_act, 1)
            tile(0, True)
            act.wait_ge(dense_act, 1)
            act.wait_ge(mlp_loaded, 16 * MLP_LOADS)
            with act.Fori(1, TILES) as t:
                tile(t, False)
            mlp_input(TILES - 1, last=True)
            for m in range(0, M1, 2):
                act.wait_ge(last_h1_mm, m + 1)
                nc.scalar.activation(h1[:, m, :], last_h1_ps[m][:, 0:P], ACT.Relu, bias=bt1[:, m:m + 1])\
                  .then_inc(last_h1_act, 1)
            act.wait_ge(last_h2_mm, 1)
            nc.scalar.activation(h2[:, 0, :], last_h2_ps[0][:, 0:P], ACT.Relu, bias=bt2[:, 0:1]).then_inc(last_h2_act, 1)
            mlp_output(TILES - 1)

        @block.vector
        def _(dve):
            def correct_x(s, which):
                dve.wait_ge(corrX_loaded[s], 16 * LOADS_HALF)
                v = VX[:, s, :, :]
                nc.vector.tensor_tensor(v, v, corrX[:, s, which, :, :], ALU.add).then_inc(v_x, 1)
                dve.wait_ge(v_x, 2 * s + which + 1)

            def correct_own(which):
                dve.wait_ge(corrO_loaded, 16 * 4 * LOADS_QUARTER)
                nc.vector.tensor_tensor(VO[:, :, :], VO[:, :, :], corrO[:, which, :, :], ALU.add).then_inc(v_own, 1)
                dve.wait_ge(v_own, which + 1)

            def transpose_half(t, s, slot, gathers):
                for g in range(2 * s, 2 * s + 2):
                    dve.wait_ge(gathered[slot][g], gathers)
                    nc.vector.transpose(view(ET, g * EXT * BB, [[1, QTR * BB]]), emb[:, slot, g * QTR * D:(g + 1) * QTR * D])
                    last = nc.vector.transpose(view(ET, (g * EXT + QTR) * BB, [[1, ROT * BB]]),
                                               emb[:, slot, g * QTR * D:(g * QTR + ROT) * D])
                last.then_inc(et_ready, 1)
                dve.wait_ge(et_ready, 2 * t + s + 1)

            def products(u, ring, s):
                o, zo = u * UB, ring * UB * 2 * PAIRS + s * PAIRS
                for v in range(2):
                    eo = (2 * s + v) * EXT * BB + o
                    nc.vector.tensor_tensor(view(z, zo + v * QPAIRS, [[2 * PAIRS, UB], [QTR, ROT], [1, QTR]]),
                                            view(ET, eo, [[1, UB], [0, ROT], [BB, QTR]]),
                                            view(ET, eo + BB, [[1, UB], [BB, ROT], [BB, QTR]]), ALU.mult)
                eo = 2 * s * EXT * BB + o
                nc.vector.tensor_tensor(view(z, zo + OWN, [[2 * PAIRS, UB], [QTR, QTR], [1, QTR]]),
                                        view(ET, eo, [[1, UB], [BB, QTR], [0, QTR]]),
                                        view(ET, eo + EXT * BB, [[1, UB], [0, QTR], [BB, QTR]]), ALU.mult)\
                  .then_inc(z_ready[s], 1)

            def empty(u, c, group):
                col = (u * UB + c * GB) * Q
                dve.wait_ge(t_formed, group)
                nc.vector.tensor_copy(*own_copy(1, c, col))
                nc.vector.tensor_copy(*x_copy(1, c, col)).then_inc(t_dve, 1)

            def tile(t, slot, gathers, first):
                if not first:
                    dve.wait_ge(e_ready, t * UNITS)
                if first:
                    for s in range(2):
                        transpose_half(t, s, slot, gathers)
                        for u in range(2):
                            products(u, u, s)
                else:
                    for s in range(2):
                        transpose_half(t, s, slot, gathers)
                    for u in range(2):
                        dve.wait_ge(t_formed, 2 * (t * UNITS + u) - 2)
                        for s in range(2):
                            products(u, u, s)
                if first:
                    for s, r in ((0, 0), (0, 1), (1, 0)):
                        dve.wait_ge(half_stored[s][r], 16 * STORES_PART)
                for u in range(UNITS):
                    if u >= 2:
                        dve.wait_ge(t_formed, 2 * (t * UNITS + u) - 2)
                        for s in range(2):
                            products(u, u % 2, s)
                    if u >= 1:
                        for c in range(2):
                            empty(u - 1, c, 2 * (t * UNITS + u - 1) + c + 1)
                            if first and u == UNITS - 1:
                                dve.wait_ge(setup_act, act_banks(N_SETUP - 1))
                                correct_x(0, c)
                for c in range(2):
                    empty(UNITS - 1, c, 2 * (t * UNITS + UNITS - 1) + c + 1)
                if first:
                    correct_x(1, 0)
                    correct_x(1, 1)
                    correct_own(0)
                    correct_own(1)

            nc.vector.memset(w0pair[:, :, :], 0.0).then_inc(w0pair_zero, 1)
            nc.vector.memset(E[:, :, :, :], 0.0).then_inc(E_zero, 1)
            dve.wait_ge(setup_act, 1)
            dve.wait_ge(setup_mm, 2)
            for s in range(2):
                first, second = (view(w0T, HALF, [[F, HALF], [1, HALF]]), view(setup_ps[1], 0, [[1, HALF], [F, HALF]]))
                if s == 1:
                    first, second = (view(w0T, HALF, [[1, HALF], [F, HALF]]), view(setup_ps[1], 0, [[F, HALF], [1, HALF]]))
                nc.vector.tensor_tensor(w0x[:, s, :, :], first, second, ALU.add).then_inc(w0x_ready, 1)
            nc.vector.tensor_copy(w0T[:, BANK:2 * BANK], setup_ps[1][:, :]).then_inc(setup_dve, 1)
            dve.wait_ge(setup_dve, 1)
            for u in range(2):
                last = nc.vector.tensor_tensor(
                    view(w0xq, u * QTR * QTR, [[2 * QTR * QTR, 2], [QTR, QTR], [1, QTR]]),
                    view(w0T, u * QTR * F + (1 - u) * QTR, [[HALF * (F + 1), 2], [F, QTR], [1, QTR]]),
                    view(w0T, (1 - u) * QTR * F + u * QTR, [[HALF * (F + 1), 2], [1, QTR], [F, QTR]]), ALU.add)
            last.then_inc(w0x_ready, 1)
            for q0, q1 in ((0, QTR), (QTR, EXT)):
                last = nc.vector.tensor_tensor(
                    view(w0sym, q0, [[QTR * EXT, 4], [EXT, QTR], [1, q1 - q0]]),
                    view(w0T, 0, [[QTR * (F + 1), 4], [F, QTR], [1, q1 - q0]]),
                    view(w0T, 0, [[QTR * (F + 1), 4], [1, QTR], [F, q1 - q0]]), ALU.add)
            last.then_inc(w0sym_ready, 1)
            dve.wait_ge(w0sym_ready, 1)
            dve.wait_ge(w0x_ready, 3)
            dve.wait_ge(w0pair_zero, 1)
            for s in range(2):
                nc.vector.tensor_copy(view(w0pair, s * PAIRS, [[QPAIRS, 2], [QTR, ROT - 1], [1, QTR]]),
                                      view(w0sym, 2 * s * QTR * EXT + 1, [[QTR * EXT, 2], [1, ROT - 1], [EXT + 1, QTR]]))
            nc.vector.tensor_copy(view(w0pair, QTR * (ROT - 1), [[PAIRS, 2], [QPAIRS, 2], [1, ROT]]),
                                  view(w0sym, ROT, [[2 * QTR * EXT, 2], [QTR * EXT, 2], [EXT + 1, ROT]]))
            nc.vector.tensor_copy(w0pair[:, :, OWN:PAIRS], view(w0xq, 0, [[2 * QTR * QTR, 2], [1, QTR * QTR]]))\
              .then_inc(w0pair_ready, 1)
            nc.vector.memset(corrX[0:OWN, :, 1, :, :], 0.0).then_inc(corr_zero, 1)
            nc.vector.memset(corrO[:, :, :, :], 0.0).then_inc(corr_zero, 1)
            nc.vector.memset(corrS[:, :, :], 0.0).then_inc(corr_zero, 1)
            tile(0, 0, 16 * QTR, True)
            tile(1, 1, 16 * QTR, False)
            with dve.Fori(1, TILES // EMB_RING) as i:
                for slot in range(EMB_RING):
                    tile(i * EMB_RING + slot, slot, (i + 1) * (16 * QTR), False)
            dve.wait_ge(mlp_loaded, 16 * MLP_LOADS)
            for m in range(1, M1, 2):
                dve.wait_ge(last_h1_mm, m + 1)
                nc.vector.tensor_scalar(h1[:, m, :], last_h1_ps[m][:, 0:P], bt1[:, m:m + 1], 0.0, ALU.add, ALU.max)\
                  .then_inc(last_h1_dve, 1)
            dve.wait_ge(last_h2_mm, 1)
            nc.vector.tensor_scalar(h2[:, 1, :], last_h2_ps[1][:, 0:P], bt2[:, 1:2], 0.0, ALU.add, ALU.max)\
              .then_inc(last_h2_dve, 1)

        @block.tensor
        def _(pe):
            def setup_bank(n):
                if n - 6 == 1:
                    pe.wait_ge(setup_dve, 1)
                elif n >= 6:
                    pe.wait_ge(setup_act, act_banks(n - 6))
                return setup_ps[n % 6]

            def w1_fields(h):
                return w1[:, h:h + WPB, :].rearrange("m w j -> m (w j)")

            def form_pairs(ring, c):
                for b in range(GB):
                    bb = c * GB + b
                    for s in range(2):
                        last = nc.tensor.matmul(pair_ps[s][c][0:PAIRS, b * Q * F:(b + 1) * Q * F],
                                                z[:, ring, bb, s * PAIRS:(s + 1) * PAIRS], E[:, ring, bb, :],
                                                start=True, stop=True)
                return last

            def form_squares(ring, c):
                for b in range(GB):
                    bb = c * GB + b
                    for half in range(2):
                        for g in range(2):
                            row = 32 * (2 * g + half)
                            last = nc.tensor.matmul(
                                sg_ps[c][row:row + F, b * Q * HALF:(b + 1) * Q * HALF], z2[:, ring, bb, g * F:(g + 1) * F],
                                view(E, (ring * UB + bb) * Q * F + half * HALF, [[F, Q], [1, HALF]]),
                                start=True, stop=True)
                return last

            def form(u, t, first):
                ring = u % 2
                for s in range(2):
                    pe.wait_ge(z_ready[s], t * UNITS + u + 1)
                pe.wait_ge(e_ready, t * UNITS + u + 1)
                for c in range(2):
                    if first and u == 0:
                        pe.wait_ge(setup_act, act_banks(N_SETUP - 4 + 3 * c))
                    else:
                        pe.wait_ge(t_act, 2 * (t * UNITS + u) + c - 1)
                        pe.wait_ge(t_dve, 2 * (t * UNITS + u) + c - 1)
                    for form_part in ((form_pairs, form_squares), (form_squares, form_pairs))[c]:
                        last = form_part(ring, c)
                    last.then_inc(t_formed, 1)

            def contract(t, wait_v, between):
                def t_part(offset):
                    return view(T, offset, [[1, P]])
                out1, out2 = acc_ps[:, 0:P], acc_ps[:, P:2 * P]
                pe.wait_ge(sg_emptied, 2 * UNITS * (t + 1))
                if wait_v:
                    pe.wait_ge(w0g_loaded, 16 * 4)
                for h in range(QTR):
                    nc.tensor.matmul(out1, W0g[:, h, :], t_part(TSG + (QTR + h) * P), start=(h == 0), stop=(h == QTR - 1))
                def contract_x(s):
                    if wait_v:
                        pe.wait_ge(v_x, 2 * (s + 1))
                    for h in range(HALF):
                        nc.tensor.matmul(out2, VX[:, s, h, :], t_part(TX + (s * HALF + h) * P),
                                         start=(s == 0 and h == 0), stop=False)

                pe.wait_ge(t_act, 2 * UNITS * (t + 1))
                pe.wait_ge(t_dve, 2 * UNITS * (t + 1))
                contract_x(0)
                if between:
                    between()
                contract_x(1)
                if wait_v:
                    pe.wait_ge(v_own, 2)
                for h in range(HALF):
                    nc.tensor.matmul(out2, VO[:, h, :], t_part(TOWN + h * P), start=False, stop=False)
                if wait_v:
                    pe.wait_ge(v_squares, 1)
                for h in range(QTR):
                    last = nc.tensor.matmul(out2, VS[:, h, :], t_part(TSG + h * P), start=False, stop=(h == QTR - 1))
                last.then_inc(acc_ready, 1)

            def mlp1(t):
                pe.wait_ge(x_ready, t + 1)
                for m in range(M1):
                    o = hid_ps[:, m * P:(m + 1) * P]
                    for k in range(2):
                        nc.tensor.matmul(o, wt1[:, k, m * P:(m + 1) * P], x[:, k, :], start=(k == 0), stop=False)
                    last = nc.tensor.matmul(o, wt1d[:, m * P:(m + 1) * P], xd[:, :], start=False, stop=True)
                last.then_inc(h1_mm, 1)

            def mlp2(t):
                pe.wait_ge(h1_ready, t + 1)
                for m in range(M2):
                    for k in range(M1):
                        last = nc.tensor.matmul(hid_ps[:, m * P:(m + 1) * P], wt2[:, k, m * P:(m + 1) * P],
                                                h1[:, k, :], start=(k == 0), stop=(k == M1 - 1))
                last.then_inc(h2_mm, 1)

            def mlp3(t):
                pe.wait_ge(h2_ready, t + 1)
                for k in range(M2):
                    last = nc.tensor.matmul(hid_ps[0:1, 0:P], wt3[:, k:k + 1], h2[:, k, :], start=(k == 0), stop=(k == M2 - 1))
                last.then_inc(y_mm, 1)

            def last_mlp():
                t = TILES - 1
                for m in range(M1):
                    nc.tensor.matmul(last_h1_ps[m][:, 0:P], wt1d[:, m * P:(m + 1) * P], denseT[:, t * P:(t + 1) * P],
                                     start=True, stop=False)
                pe.wait_ge(x_ready, t + 1)
                for m in range(M1):
                    for k in range(2):
                        last = nc.tensor.matmul(last_h1_ps[m][:, 0:P], wt1[:, k, m * P:(m + 1) * P], x[:, k, :],
                                                start=False, stop=(k == 1))
                    last.then_inc(last_h1_mm, 1)
                for k in range(M1):
                    if k % 2 == 0:
                        pe.wait_ge(last_h1_act, k // 2 + 1)
                    else:
                        pe.wait_ge(last_h1_dve, k // 2 + 1)
                    for m in range(M2):
                        last = nc.tensor.matmul(last_h2_ps[m][:, 0:P], wt2[:, k, m * P:(m + 1) * P], h1[:, k, :],
                                                start=(k == 0), stop=(k == M1 - 1))
                last.then_inc(last_h2_mm, 1)
                pe.wait_ge(last_h2_act, 1)
                pe.wait_ge(last_h2_dve, 1)
                for k in range(M2):
                    last = nc.tensor.matmul(hid_ps[0:1, 0:P], wt3[:, k:k + 1], h2[:, k, :], start=(k == 0), stop=(k == M2 - 1))
                last.then_inc(y_mm, 1)

            pe.wait_ge(ident_loaded, 16)
            for n in range(N_W0T):
                pe.wait_ge(w0_loaded[n], 16)
                for i in range(BANK // P):
                    last = nc.tensor.transpose(setup_ps[n][:, i * P:(i + 1) * P], w0[:, n * (BANK // P) + i, :], ident[:, :])
                last.then_inc(setup_mm, 1)
            for s in range(2):
                pe.wait_ge(w0x_ready, s + 1)
                for r in range(2):
                    for w in range(HALF // WPB):
                        if r == 0:
                            pe.wait_ge(w1_loaded[s * (HALF // WPB) + w], 16)
                        nc.tensor.matmul(setup_bank(cross_bank(s, r, w))[:, :],
                                         w0x[:, s, r * QTR:(r + 1) * QTR, :].rearrange("m o t -> m (o t)"),
                                         w1_fields(s * HALF + w * WPB), start=True, stop=True).then_inc(setup_mm, 1)
                pe.wait_ge(w0x_ready, 3)
                for w in range(QUARTER_BANKS):
                    ps = setup_bank(quarter_bank(s, w))
                    for u in range(2):
                        last = nc.tensor.matmul(ps[64 * u:64 * u + 64, :], w0xq[:, s, u, :, :].rearrange("m o t -> m (o t)"),
                                                w1_fields((2 * s + u) * QTR + w * WPB), start=True, stop=True)
                    last.then_inc(setup_mm, 1)
            pe.wait_ge(w0pair_ready, 1)
            for s in range(2):
                for w in range(HALF // WPB):
                    nc.tensor.matmul(setup_bank(N_X + s * (HALF // WPB) + w)[:, :], w0pair[:, s, :],
                                     w1_fields((1 - s) * HALF + w * WPB), start=True, stop=True).then_inc(setup_mm, 1)
            pe.wait_ge(dense_loaded, 16 * TILES)
            for t in range(TILES):
                last = nc.tensor.transpose(hid_ps[0:NX, t * P:(t + 1) * P], dense_in[:, t, :], ident[:, :])
            last.then_inc(dense_mm, 1)
            for w in range(HALF // WPB):
                ps = setup_bank(N_OWN + w)
                for s in range(2):
                    last = nc.tensor.matmul(ps[s * OWN:(s + 1) * OWN, :], w0pair[:, s, 0:OWN],
                                            w1_fields(s * HALF + w * WPB), start=True, stop=True)
                last.then_inc(setup_mm, 1)
            pe.wait_ge(setup_dve, 1)
            pe.wait_ge(dense_act, 1)
            for w, ps in enumerate(squares_ps):
                for j, quarter in enumerate(QUARTER_OF_BLOCK):
                    last = nc.tensor.matmul(ps[32 * j:32 * j + F, :], w0T[:, 0:F * F:F + 1],
                                            w1_fields(quarter * QTR + w * WPB), start=True, stop=True)
                last.then_inc(squares_mm, 1)

            for u in range(UNITS):
                form(u, 0, True)
            pe.wait_ge(squares_act, QTR // WPB)
            contract(0, True, None)
            pe.wait_ge(mlp_loaded, 16 * MLP_LOADS)
            with pe.Fori(1, TILES) as t:
                form(0, t, False)
                form(1, t, False)
                mlp1(t - 1)
                form(2, t, False)
                form(3, t, False)
                mlp2(t - 1)
                contract(t, False, lambda: mlp3(t - 1))
            last_mlp()


def kernel(**inputs):
    import numpy as np
    import concourse.bacc as bacc
    from concourse.bass_utils import run_bass_kernel_spmd

    nc = bacc.Bacc("TRN2", target_bir_lowering=False, num_devices=1)
    arrays = {}

    def given(name, array):
        array = np.ascontiguousarray(array)
        arrays[name] = array
        return nc.dram_tensor(name, array.shape, mybir.dt.from_np(array.dtype), kind="ExternalInput").ap()

    ids = given("ids_in", inputs["ids"])
    tables = [given(f"tbl_{f}_in", inputs[f"tbl_{f}"]) for f in range(F)]
    by_partition = {name: np.asarray(inputs[name]).reshape(-1, P).T for name in ("b_top1", "b_top2", "W_top3")}
    args = [given(name + "_in", by_partition.get(name, inputs[name])) for name in
            ("L0_rec_W0", "L0_rec_W1", "W_top1", "b_top1", "W_top2", "b_top2", "W_top3", "dense_ctx")]
    identity = given("identity_in", np.eye(P, dtype=np.float32))
    out = nc.dram_tensor("out_y", (ids.shape[0], 1), mybir.dt.float32, kind="ExternalOutput").ap()
    scratch = [nc.dram_tensor(f"cross_scratch{s}", (2 * EXT, 2 * EXT, HALF, C), mybir.dt.float32, kind="Internal").ap()
               for s in range(2)]
    scratch_q = [nc.dram_tensor(f"cross_scratch_quarter{g}", (EXT, EXT, QTR, C), mybir.dt.float32, kind="Internal").ap()
                 for g in range(4)]
    build(nc, ids, tables, *args, identity, out, scratch, scratch_q)
    result = run_bass_kernel_spmd(nc, [arrays], core_ids=[0])
    return result.results[0]["out_y"]
```
